# Optimizing a Trainium2 kernel written in Bass

```python
import numpy as np
import jax
import jax.numpy as jnp

def _softmax(x, axis=-1):
    return jax.nn.softmax(x, axis=axis)

def _gelu(x):
    return jax.nn.gelu(x, approximate=True)

def _silu(x):
    return jax.nn.silu(x)

def _sigmoid(x):
    return jax.nn.sigmoid(x)

def _layernorm(x, axis=-1, eps=1e-05):
    m = jnp.mean(x, axis=axis, keepdims=True)
    v = jnp.var(x, axis=axis, keepdims=True)
    return (x - m) / jnp.sqrt(v + eps)

def _scatter_add(tgt, idx, src, axis=0):
    return tgt.at[idx].add(src)

def _segment_sum(src, seg, n):
    return jax.ops.segment_sum(src, seg, n)
kernel_name = 'mk_prb_d1_jaxref_r4_495c89'

def setup_inputs(seed: int=0):
    np.random.seed(seed)
    _w = jnp.asarray

    def _L0_attn_setup():
        import jax, jax.numpy as jnp
        import numpy as np
        EPS = 1e-05
        CHUNK = 128

        def lightning_attn(q, k, v, ld, chunk=CHUNK):
            b, n, h, d = q.shape
            nc = n // chunk
            idx = jnp.arange(chunk)
            diff = idx[:, None] - idx[None, :]
            mask = diff >= 0
            D = jnp.exp(ld[:, None, None] * jnp.where(mask, diff, 0)) * mask
            q_decay = jnp.exp(ld[None, :] * (idx + 1)[:, None])
            k_decay = jnp.exp(ld[None, :] * (chunk - 1 - idx)[:, None])
            chunk_decay = jnp.exp(ld * chunk)
            qc = jnp.moveaxis(q.reshape(b, nc, chunk, h, d), 1, 0)
            kc = jnp.moveaxis(k.reshape(b, nc, chunk, h, d), 1, 0)
            vc = jnp.moveaxis(v.reshape(b, nc, chunk, h, d), 1, 0)

            def step(S, inp):
                qb, kb, vb = inp
                scores = jnp.einsum('bchd,bshd->bhcs', qb, kb) * D[None]
                o_intra = jnp.einsum('bhcs,bshd->bchd', scores, vb)
                o_inter = jnp.einsum('bchd,bhde->bche', qb, S) * q_decay[None, :, :, None]
                S_new = chunk_decay[None, :, None, None] * S + jnp.einsum('bshd,bshe->bhde', kb * k_decay[None, :, :, None], vb)
                return (S_new, o_intra + o_inter)
            S0 = jnp.zeros((b, h, d, d), dtype=q.dtype)
            S_final, oc = jax.lax.scan(step, S0, (qc, kc, vc))
            out = jnp.moveaxis(oc, 0, 1).reshape(b, n, h, d)
            return (out, S_final)

        def group_rmsnorm_fused_gate(o, gate, w, num_heads):
            b, n, d = o.shape
            hd = d // num_heads
            o = o * jax.nn.sigmoid(gate)
            og = o.reshape(b, n, num_heads, hd)
            og = og * jax.lax.rsqrt(jnp.mean(og * og, axis=-1, keepdims=True) + EPS)
            return og.reshape(b, n, d) * w
        key = jax.random.key(seed)
        ks = jax.random.split(key, 10)
        B, N, D, H = (2, 1024, 512, 16)
        HD = D // H
        s = 1.0 / np.sqrt(D)
        x = jax.random.normal(ks[0], (B, N, D), dtype=jnp.float32)
        log_decay = -jax.random.uniform(ks[1], (H,), dtype=jnp.float32, minval=0.01, maxval=1.0)
        Wq = jax.random.normal(ks[2], (D, D), dtype=jnp.float32) * s
        Wk = jax.random.normal(ks[3], (D, D), dtype=jnp.float32) * s
        Wv = jax.random.normal(ks[4], (D, D), dtype=jnp.float32) * s
        Wo = jax.random.normal(ks[5], (D, D), dtype=jnp.float32) * s
        Wg1 = jax.random.normal(ks[6], (D, HD), dtype=jnp.float32) * s
        Wg2 = jax.random.normal(ks[7], (HD, D), dtype=jnp.float32) / np.sqrt(HD)
        norm_w = jnp.ones((D,), dtype=jnp.float32)
        return {'x': x, 'log_decay': log_decay, 'Wq': Wq, 'Wk': Wk, 'Wv': Wv, 'Wo': Wo, 'Wg1': Wg1, 'Wg2': Wg2, 'norm_w': norm_w}
    _L0_attn_in = _L0_attn_setup()

    def _L0_ffn_setup():
        import jax, jax.numpy as jnp
        import numpy as np
        import math
        D_MODEL = 512
        D_FF = 2048
        NUM_EXPERTS = 8
        TOP_K = 2
        CAPACITY_FACTOR = 1.25
        BATCH, SEQ = (4, 512)

        def _moe_forward(x, Wg, w1, w2):
            B, T, d = x.shape
            S = B * T
            E, K = (NUM_EXPERTS, TOP_K)
            C = math.ceil(CAPACITY_FACTOR * S * K / E)
            xr = x.reshape(S, d)
            probs = jax.nn.softmax(xr @ Wg, axis=-1)
            gate_vals, expert_idx = jax.lax.top_k(probs, K)
            flat_e = expert_idx.reshape(-1)
            oh = jax.nn.one_hot(flat_e, E, dtype=jnp.int32)
            pos = jnp.sum((jnp.cumsum(oh, axis=0) - 1) * oh, axis=1)
            kept = pos < C
            i = jnp.arange(S * K)
            slot = i % K * S + i // K
            sentinel = S * K
            pos_w = jnp.where(kept, pos, C)
            dispatch_mask = jnp.full((E, C), sentinel, dtype=jnp.int32)
            dispatch_mask = dispatch_mask.at[flat_e, pos_w].set(slot.astype(jnp.int32), mode='drop')
            combine_weights = (gate_vals * kept.reshape(S, K)).T
            dispatched = xr[dispatch_mask.reshape(-1) % S].reshape(E, C, d)
            h = jax.nn.relu(jnp.einsum('ecd,edf->ecf', dispatched, w1))
            expert_out = jnp.einsum('ecf,efd->ecd', h, w2)
            rerouted = jnp.zeros((S * K + 1, d), dtype=expert_out.dtype)
            rerouted = rerouted.at[dispatch_mask.reshape(-1)].set(expert_out.reshape(-1, d))
            rerouted = rerouted[:-1].reshape(K, S, d)
            out = jnp.einsum('ks,ksm->sm', combine_weights, rerouted)
            return out.reshape(B, T, d)
        key = jax.random.key(seed)
        k1, k2, k3, k4 = jax.random.split(key, 4)
        x = jax.random.normal(k1, (BATCH, SEQ, D_MODEL), dtype=jnp.float32)
        Wg = jax.random.normal(k2, (D_MODEL, NUM_EXPERTS), dtype=jnp.float32) * 0.02
        w1 = jax.random.normal(k3, (NUM_EXPERTS, D_MODEL, D_FF), dtype=jnp.float32) * 0.02
        w2 = jax.random.normal(k4, (NUM_EXPERTS, D_FF, D_MODEL), dtype=jnp.float32) * 0.02
        return {'x': x, 'Wg': Wg, 'w1': w1, 'w2': w2}
    _L0_ffn_in = _L0_ffn_setup()
    _d = {'L0_attn_x': _L0_attn_in['x'], 'L0_attn_log_decay': _L0_attn_in['log_decay'], 'L0_attn_Wq': _L0_attn_in['Wq'], 'L0_attn_Wk': _L0_attn_in['Wk'], 'L0_attn_Wv': _L0_attn_in['Wv'], 'L0_attn_Wo': _L0_attn_in['Wo'], 'L0_attn_Wg1': _L0_attn_in['Wg1'], 'L0_attn_Wg2': _L0_attn_in['Wg2'], 'L0_attn_norm_w': _L0_attn_in['norm_w'], 'L0_ffn_Wg': _L0_ffn_in['Wg'], 'L0_ffn_w1': _L0_ffn_in['w1'], 'L0_ffn_w2': _L0_ffn_in['w2']}
    _x0 = _d['L0_attn_x']
    _d['L0_attn_x'] = jax.random.normal(jax.random.fold_in(jax.random.key(seed), 1), (4, 1024, 512), dtype=_x0.dtype)
    del _x0
    return _d

def reference(L0_attn_x, L0_attn_log_decay, L0_attn_Wq, L0_attn_Wk, L0_attn_Wv, L0_attn_Wo, L0_attn_Wg1, L0_attn_Wg2, L0_attn_norm_w, L0_ffn_Wg, L0_ffn_w1, L0_ffn_w2):

    def _L0_attn_ref(x, log_decay, Wq, Wk, Wv, Wo, Wg1, Wg2, norm_w):
        import jax, jax.numpy as jnp
        import numpy as np
        EPS = 1e-05
        CHUNK = 128

        def lightning_attn(q, k, v, ld, chunk=CHUNK):
            b, n, h, d = q.shape
            nc = n // chunk
            idx = jnp.arange(chunk)
            diff = idx[:, None] - idx[None, :]
            mask = diff >= 0
            D = jnp.exp(ld[:, None, None] * jnp.where(mask, diff, 0)) * mask
            q_decay = jnp.exp(ld[None, :] * (idx + 1)[:, None])
            k_decay = jnp.exp(ld[None, :] * (chunk - 1 - idx)[:, None])
            chunk_decay = jnp.exp(ld * chunk)
            qc = jnp.moveaxis(q.reshape(b, nc, chunk, h, d), 1, 0)
            kc = jnp.moveaxis(k.reshape(b, nc, chunk, h, d), 1, 0)
            vc = jnp.moveaxis(v.reshape(b, nc, chunk, h, d), 1, 0)

            def step(S, inp):
                qb, kb, vb = inp
                scores = jnp.einsum('bchd,bshd->bhcs', qb, kb) * D[None]
                o_intra = jnp.einsum('bhcs,bshd->bchd', scores, vb)
                o_inter = jnp.einsum('bchd,bhde->bche', qb, S) * q_decay[None, :, :, None]
                S_new = chunk_decay[None, :, None, None] * S + jnp.einsum('bshd,bshe->bhde', kb * k_decay[None, :, :, None], vb)
                return (S_new, o_intra + o_inter)
            S0 = jnp.zeros((b, h, d, d), dtype=q.dtype)
            S_final, oc = jax.lax.scan(step, S0, (qc, kc, vc))
            out = jnp.moveaxis(oc, 0, 1).reshape(b, n, h, d)
            return (out, S_final)

        def group_rmsnorm_fused_gate(o, gate, w, num_heads):
            b, n, d = o.shape
            hd = d // num_heads
            o = o * jax.nn.sigmoid(gate)
            og = o.reshape(b, n, num_heads, hd)
            og = og * jax.lax.rsqrt(jnp.mean(og * og, axis=-1, keepdims=True) + EPS)
            return og.reshape(b, n, d) * w
        b, n, d = x.shape
        H = log_decay.shape[0]
        hd = d // H
        q = jax.nn.silu(jnp.einsum('bnd,de->bne', x, Wq).reshape(b, n, H, hd))
        k = jax.nn.silu(jnp.einsum('bnd,de->bne', x, Wk).reshape(b, n, H, hd))
        v = jax.nn.silu(jnp.einsum('bnd,de->bne', x, Wv).reshape(b, n, H, hd))
        o, _ = lightning_attn(q, k, v, log_decay)
        o = o.reshape(b, n, d)
        gate = jnp.einsum('bnk,kd->bnd', jnp.einsum('bnd,dk->bnk', x, Wg1), Wg2)
        o = group_rmsnorm_fused_gate(o, gate, norm_w, H)
        return jnp.einsum('bnd,de->bne', o, Wo)

    def _L0_ffn_ref(x, Wg, w1, w2):
        import jax, jax.numpy as jnp
        import numpy as np
        import math
        D_MODEL = 512
        D_FF = 2048
        NUM_EXPERTS = 8
        TOP_K = 2
        CAPACITY_FACTOR = 1.25
        BATCH, SEQ = (4, 512)

        def _moe_forward(x, Wg, w1, w2):
            B, T, d = x.shape
            S = B * T
            E, K = (NUM_EXPERTS, TOP_K)
            C = math.ceil(CAPACITY_FACTOR * S * K / E)
            xr = x.reshape(S, d)
            probs = jax.nn.softmax(xr @ Wg, axis=-1)
            gate_vals, expert_idx = jax.lax.top_k(probs, K)
            flat_e = expert_idx.reshape(-1)
            oh = jax.nn.one_hot(flat_e, E, dtype=jnp.int32)
            pos = jnp.sum((jnp.cumsum(oh, axis=0) - 1) * oh, axis=1)
            kept = pos < C
            i = jnp.arange(S * K)
            slot = i % K * S + i // K
            sentinel = S * K
            pos_w = jnp.where(kept, pos, C)
            dispatch_mask = jnp.full((E, C), sentinel, dtype=jnp.int32)
            dispatch_mask = dispatch_mask.at[flat_e, pos_w].set(slot.astype(jnp.int32), mode='drop')
            combine_weights = (gate_vals * kept.reshape(S, K)).T
            dispatched = xr[dispatch_mask.reshape(-1) % S].reshape(E, C, d)
            h = jax.nn.relu(jnp.einsum('ecd,edf->ecf', dispatched, w1))
            expert_out = jnp.einsum('ecf,efd->ecd', h, w2)
            rerouted = jnp.zeros((S * K + 1, d), dtype=expert_out.dtype)
            rerouted = rerouted.at[dispatch_mask.reshape(-1)].set(expert_out.reshape(-1, d))
            rerouted = rerouted[:-1].reshape(K, S, d)
            out = jnp.einsum('ks,ksm->sm', combine_weights, rerouted)
            return out.reshape(B, T, d)
        return _moe_forward(x, Wg, w1, w2)
    x = L0_attn_x
    xn = _layernorm(x, axis=-1)
    x = x + _L0_attn_ref(xn, L0_attn_log_decay, L0_attn_Wq, L0_attn_Wk, L0_attn_Wv, L0_attn_Wo, L0_attn_Wg1, L0_attn_Wg2, L0_attn_norm_w) + _L0_ffn_ref(xn, L0_ffn_Wg, L0_ffn_w1, L0_ffn_w2)
    return x

_drawn_inputs = setup_inputs


def setup_inputs(seed=0):
    import zlib

    import numpy as np

    out = dict(_drawn_inputs(seed))
    spreads = {'L0_attn_norm_w': (1.0, 0.2)}
    factors = {}
    for name, (base, spread) in spreads.items():
        noise = np.random.default_rng([zlib.crc32(name.encode()), seed]).standard_normal(out[name].shape)
        drawn = base * np.exp(spread * noise) if base else spread * noise
        out[name] = jnp.asarray(drawn.astype(out[name].dtype))
    for name, factor in factors.items():
        out[name] = (out[name] * factor).astype(out[name].dtype)
    return out
```

```python
from contextlib import ExitStack

import concourse.bass as bass
import numpy as np
from concourse import mybir

F32 = mybir.dt.float32
F32R = mybir.dt.float32r
BF16 = mybir.dt.bfloat16
I32 = mybir.dt.int32
U32 = mybir.dt.uint32
ALU = mybir.AluOpType
ACT = mybir.ActivationFunctionType
AX = mybir.AxisListType

P = 128
BATCH, SEQ, D = 4, 1024, 512
TOKENS = BATCH * SEQ
TILES = TOKENS // P
CHUNKS = SEQ // P
DT = D // P
HEADS, HD = 16, 32
HPG = P // HD
GROUPS = HEADS // HPG
EPS = 1e-5

EXPERTS, TOP, FF = 8, 2, 2048
CAP = -(-5 * TOKENS * TOP // (4 * EXPERTS))
SLOT_TILES = CAP // P
FT = FF // P
FPC = 4
FCHUNKS = FT // FPC
BLOCKS = [4, 3, 3]
STARTS = [0, 4, 7]
REC = 2 + EXPERTS
PAD_ROWS = max(BLOCKS) * P
DROPPED = 2 * EXPERTS * CAP
UNITS = 8
UNITS_PER_EXPERT = 2 * FT
WEIGHT_UNITS = 4 * DT


def build(nc, x, log_decay, wq, wk, wv, wo, wg1, wg2, norm_w, w_route, w1, w2, out):
    assert sum(BLOCKS) * P == CAP and CAP % P == 0
    xn_dram = nc.dram_tensor("xn_rows", (TOKENS, D), F32, kind="Internal").ap()
    table = nc.dram_tensor("slot_table", (EXPERTS * CAP, REC), F32, kind="Internal").ap()
    x_rows = x.rearrange("b n d -> (b n) d")
    slots_of = table.rearrange("(e p j) r -> e p j r", e=EXPERTS, j=SLOT_TILES)

    with ExitStack() as ctx:
        attention_only, experts_only = ExitStack(), ExitStack()

        def sb(name, shape, dt=F32, where=ctx):
            return where.enter_context(nc.sbuf_tensor(name, shape, dt))

        def sem(name):
            return ctx.enter_context(nc.semaphore(name))

        ident = sb("ident", [P, P])
        raw = sb("raw_weights", [P, UNITS, D])
        w1_hi, w1_lo, w2_hi, w2_lo = ([None] * FCHUNKS for _ in range(4))

        def ffn_chunk(c, where):
            for name, parts in (("w1_hi", w1_hi), ("w1_lo", w1_lo), ("w2_hi", w2_hi), ("w2_lo", w2_lo)):
                parts[c] = sb(f"{name}{c}", [P, FPC, D], F32R, where)

        ffn_chunk(0, ctx)
        xg = sb("gathered", [P, 2, D])
        slot_rec = sb("slot_rec", [P, SLOT_TILES, REC])
        gather_row = sb("gather_row", [P, SLOT_TILES], I32)
        add_row = sb("add_row", [P, SLOT_TILES], I32)
        slot_exp = sb("slot_exp", [P, SLOT_TILES, REC - 1])
        slot_sum = sb("slot_sum", [P, SLOT_TILES])
        slot_gate = sb("slot_gate", [P, SLOT_TILES])
        y_attn = sb("y_attn", [P, D])

        def asb(name, shape, dt=F32):
            return sb(name, shape, dt, attention_only)

        WSET = ("q", "k", "v", "o")
        w_hi = {n: asb(f"w{n}_hi", [P, DT, D], F32R) for n in WSET}
        w_lo = {n: asb(f"w{n}_lo", [P, DT, D], F32R) for n in WSET}
        small_raw = asb("small_raw", [P, DT, HD + EXPERTS])
        small_hi = asb("small_hi", [P, DT, HD + EXPERTS], F32R)
        small_lo = asb("small_lo", [P, DT, HD + EXPERTS], F32R)
        logitsT = asb("logitsT", [HD + EXPERTS, P])
        g2_raw = asb("wg2_raw", [HD, D])
        g2_hi = asb("wg2_hi", [HD, D], F32R)
        g2_lo = asb("wg2_lo", [HD, D], F32R)
        norm_col = asb("norm_col", [P, DT])
        ld_row = asb("ld_row", [P, HEADS])
        ld_col = asb("ld_col", [P, GROUPS])
        steps_left = asb("steps_left", [P, 1])
        col_plus1 = asb("col_plus1", [P, P])
        diff = asb("diff", [P, P])
        intra_decay = asb("intra_decay", [P, HPG, GROUPS, P])
        q_decay = asb("q_decay", [P, GROUPS, P])
        k_decay = asb("k_decay", [P, HEADS])
        chunk_decay = asb("chunk_decay", [P, GROUPS])
        same_head = asb("same_head", [P, P])
        before = asb("before", [P, P], BF16)
        ones = asb("ones", [P, P], BF16)
        ones_f = asb("ones_f", [P, P])
        expert_no = asb("expert_no", [P, EXPERTS])
        minus_half = asb("minus_half", [P, HEADS])
        x_ring = asb("x_ring", [P, 4, D])
        stats = asb("stats", [P, 6])
        moments = asb("moments", [P, 2])
        var_eps = asb("var_eps", [P, 1])
        rstd = asb("rstd", [P, 1])
        xn = asb("xn", [P, D])
        xnT_hi = asb("xnT_hi", [P, DT, P], F32R)
        xnT_lo = asb("xnT_lo", [P, DT, P], F32R)
        q = asb("q", [P, D])
        k = asb("k", [P, D])
        v = asb("v", [P, D])
        kd = asb("kd", [P, D])
        qT = asb("qT", [P, GROUPS, P])
        qdT = asb("qdT", [P, GROUPS, P])
        kT = asb("kT", [P, GROUPS, P])
        scores = asb("scores", [P, HPG, GROUPS, P])
        state = asb("state", [P, GROUPS, P])
        decayed = asb("decayed", [P, GROUPS, P])
        update = asb("update", [P, GROUPS, P])
        g1T_hi = asb("g1T_hi", [HD, P], F32R)
        g1T_lo = asb("g1T_lo", [HD, P], F32R)
        tanh_g = asb("tanh_g", [P, D])
        gated = asb("gated", [P, D])
        squares = asb("squares", [P, D])
        sum_sq = asb("sum_sq", [P, HEADS])
        mean_sq = asb("mean_sq", [P, HEADS])
        head_scale = asb("head_scale", [P, HEADS])
        normed = asb("normed", [P, D])
        oT_hi = asb("oT_hi", [P, DT, P], F32R)
        oT_lo = asb("oT_lo", [P, DT, P], F32R)
        logits = asb("logits", [P, EXPERTS])
        ranked = asb("ranked", [P, 8])
        rank_no = asb("rank_no", [P, 8], U32)
        chosen_no = asb("chosen_no", [P, TOP])
        chosen = asb("chosen", [P, TOP, EXPERTS])
        takes = asb("takes", [P, EXPERTS], BF16)
        taken = asb("taken", [P, EXPERTS])
        place_of = asb("place_of", [P, EXPERTS])
        place_sel = asb("place_sel", [P, TOP, EXPERTS])
        place = asb("place", [P, TOP])
        over = asb("over", [P, TOP])
        slot_f = asb("slot_f", [P, TOP])
        slot_no = asb("slot_no", [P, TOP], I32)
        record = asb("record", [P, TOP, REC])
        attention_only.close()

        def esb(name, shape, dt=F32):
            return sb(name, shape, dt, experts_only)

        for c in range(1, FCHUNKS):
            ffn_chunk(c, experts_only)
        xT_hi = [esb(f"xT_hi{j}", [P, DT, n * P], F32R) for j, n in enumerate(BLOCKS)]
        xT_lo = [esb(f"xT_lo{j}", [P, DT, n * P], F32R) for j, n in enumerate(BLOCKS)]
        h_hi = [esb(f"h_hi{i}", [P, max(BLOCKS) * P], F32R) for i in range(2)]
        h_lo = [esb(f"h_lo{i}", [P, max(BLOCKS) * P], F32R) for i in range(2)]
        y = esb("y", [P, max(BLOCKS), D])
        experts_only.close()

        banks = [ctx.enter_context(nc.psum_tensor(f"bank{i}", [P, D], F32)) for i in range(8)]
        proj, tp, sc, o_bank, u_bank = banks[0:2], banks[2:4], banks[4:6], banks[6], banks[7]
        y_bank, xt_bank, h_bank = [banks[0], banks[1], banks[6], banks[7]], banks[2:4], banks[4:6]

        names = """waits_passed small_loaded consts_made tables_made tables_masked decay_made carry_zero
            x_loaded xn_ready xn_stored xnT_made xnT_hi_made xnT_lo_made var_ready rstd_ready
            q_projected k_projected v_projected g1_projected gate_projected
            q_ready k_ready v_ready g1_hi_made g1_lo_made tanh_ready
            q_turned k_turned q_decayed qT_ready kT_ready scored masked
            kd_ready state_ready state_decayed inter_done updated attended
            gated_ready squared mean_sq_ready head_scale_ready normed_ready
            normed_turned oT_hi_made oT_lo_made out_projected y_ready out_stored
            logits_copied logits_turned logits_read takes_ready counted counts_read slots_ready routed
            attn_w_hi attn_w_lo small_hi small_lo
            table_init pads_init dve_step act_step
            rec_loaded gather_rows_ready add_rows_ready exp_ready
            x_turned xT_hi_made xT_lo_made h_done h_hi_ready h_lo_ready adds_over
            ffn_hi ffn_lo y_done y_by_act y_by_dve""".split()
        S = {n: sem(n) for n in names}
        x_early = [sem(f"x_loaded_early{i}") for i in range(2)]
        raw_loaded = [sem(f"raw_loaded{i}") for i in range(UNITS)]
        x_gathered = [sem(f"x_gathered{i}") for i in range(2)]
        y_added = [sem(f"y_added{i}") for i in range(max(BLOCKS))]

        STARTS_AT_ONE = ("y_ready", "out_stored", "add_rows_ready", "y_by_act", "y_by_dve",
                         "adds_over")

        block = ctx.enter_context(nc.Block())

        def snap(eng, v):
            return v if isinstance(v, int) else eng.snap(v)

        def wait(eng, *pairs, plain=False):
            values = [snap(eng, v + (s in STARTS_AT_ONE)) for s, v in pairs]
            for (s, _), v in zip(pairs, values):
                eng.wait_ge(S[s] if isinstance(s, str) else s, v)
            if plain or eng in (nc.sync, nc.gpsimd):
                eng.sem_inc(S["waits_passed"], 1)

        class Steps:

            def __init__(self, eng, name):
                self.eng, self.sem, self.base, self.n = eng, S[name], 0, 0

            def begin(self, base):
                self.base, self.n = base, 0

            def __call__(self, instruction):
                instruction.then_inc(self.sem, 1)
                self.n += 1
                wait(self.eng, (self.sem, self.base + self.n), plain=True)

        STEPS_BEFORE, STEPS_TILE, STEPS_AHEAD, STEPS_NORM = 3, 0, 9, 1

        def tiles_loop(eng, body):
            with eng.Fori(0, BATCH - 1) as b:
                body.start_batch()
                with eng.Fori(0, CHUNKS) as c:
                    body(b * CHUNKS + c, b * (CHUNKS + 1) + c + 1, True, True)
            body.start_batch()
            first = (BATCH - 1) * CHUNKS
            with eng.Fori(0, CHUNKS - 2) as c:
                body(c + first, c + first + BATCH, True, True)
            for t in (TILES - 2, TILES - 1):
                body(t, t + BATCH, t < TILES - 1, False)

        def experts_loop(eng, body):
            with eng.Fori(0, EXPERTS - 1) as e:
                body(e, True)
            body(EXPERTS - 1, False)

        TURN_AT = {4: [6, 9, 12, FT - 1], 3: [8, 12, FT - 1]}

        def turns(j, follows):
            if j == len(BLOCKS) - 1 and not follows:
                return {}
            nj = (j + 1) % len(BLOCKS)
            return {f: (i, nj) for i, f in enumerate(TURN_AT[BLOCKS[nj]])}

        def split_units(j, f, follows):
            if j == 0 and f < 8:
                return [(0, 8 + 3 * f + i) for i in range(3)]
            if j == len(BLOCKS) - 1 and follows and 5 <= f < 13:
                return [(1, f - 5)]
            return []

        def unit_parts(u):
            c, i = u // 8, u % 8
            hi, lo = (w1_hi, w1_lo) if i < FPC else (w2_hi, w2_lo)
            return hi[c][:, i % FPC, :], lo[c][:, i % FPC, :]

        def unit_source(e, u):
            c, i = u // 8, u % 8
            if i < FPC:
                rows = w1.rearrange("e (t p) f -> (e t) p f", p=P)
                return rows[bass.ds(e * DT + i, 1), :, c * D:(c + 1) * D]
            rows = w2.rearrange("e (t p) d -> (e t) p d", p=P)
            return rows[bass.ds(e * FT + c * FPC + i % FPC, 1), :, :]

        @block.sync
        def _(sp):
            sp.sem_inc(S["out_stored"], 1)
            for t, arrived in enumerate((*x_early, S["x_loaded"])):
                sp.dma_start(x_ring[:, t, :], x_rows[t * P:(t + 1) * P, :]).then_inc(arrived, 16)
            sp.dma_start(small_raw[:, :, 0:HD], wg1.rearrange("(t p) n -> p t n", p=P)).then_inc(S["small_loaded"], 16)
            sp.dma_start(small_raw[:, :, HD:], w_route.rearrange("(t p) n -> p t n", p=P)).then_inc(S["small_loaded"], 16)
            sp.dma_start(g2_raw[:, :], wg2).then_inc(S["small_loaded"], 16)
            sp.dma_start(norm_col[:, :], norm_w.rearrange("(t p) -> p t", p=P),
                         allow_slow_non_contiguous=True).then_inc(S["small_loaded"], 16)
            sp.dma_start(ld_row[:, :], log_decay.partition_broadcast(P)).then_inc(S["small_loaded"], 16)
            ld_groups = log_decay.rearrange("(g h) -> h g", h=HPG)
            for h in range(HPG):
                sp.dma_start(ld_col[h * HD:(h + 1) * HD, :],
                             ld_groups[h, :].partition_broadcast(HD),
                             allow_slow_non_contiguous=True).then_inc(S["small_loaded"], 16)
            def store_xn(n):
                row = snap(sp, n * P)
                wait(sp, ("xn_ready", n + 1))
                sp.dma_start(xn_dram[bass.ds(row, P), :], xn[:, :]).then_inc(S["xn_stored"], 16)

            for u in range(WEIGHT_UNITS):
                if u == UNITS:
                    store_xn(0)
                w = (wq, wk, wv, wo)[u // DT]
                if u >= UNITS:
                    sp.wait_ge(S["attn_w_lo"], u - UNITS + 1)
                sp.dma_start(raw[:, u % UNITS, :], w[u % DT * P:(u % DT + 1) * P, :]).then_inc(raw_loaded[u % UNITS], 16)
            for u in range(UNITS):
                sp.wait_ge(S["attn_w_lo"], WEIGHT_UNITS - UNITS + u + 1)
                sp.dma_start(raw[:, u:u + 1, :], unit_source(0, u).rearrange("o p n -> p o n")).then_inc(raw_loaded[u], 16)

            store_xn(1)

            def tile(t):
                slot, x_row = snap(sp, (t + 3) & 3), snap(sp, (t + 3) * P)
                wait(sp, ("x_loaded", 16 * t + 16))
                wait(sp, ("y_ready", t))
                sp.dma_start(x_ring[:, bass.ds(slot, 1), :],
                             x_rows[bass.ds(x_row, P), :].unsqueeze(1)).then_inc(S["x_loaded"], 16)
                store_xn(t + 2)
                row = snap(sp, t * P)
                wait(sp, ("y_ready", t + 1))
                sp.dma_start(out[bass.ds(row, P), :], y_attn[:, :]).then_inc(S["out_stored"], 16)

            with sp.Fori(0, TILES - 3) as t:
                tile(t)
            store_xn(TILES - 1)
            for t in range(TILES - 3, TILES):
                wait(sp, ("y_ready", t + 1))
                sp.dma_start(out[t * P:(t + 1) * P, :], y_attn[:, :]).then_inc(S["out_stored"], 16)

            sp.wait_ge(S["routed"], 16 * TOP * TILES)
            sp.dma_start(slot_rec[:, :, :], slots_of[0]).then_inc(S["rec_loaded"], 16)

            def expert(e, follows):
                def load(de, u):
                    source = unit_source(snap(sp, e + de), u)
                    wait(sp, ("ffn_lo", UNITS_PER_EXPERT * e + UNITS_PER_EXPERT * de + u - UNITS + 1))
                    sp.wait_ge(S["attn_w_lo"], WEIGHT_UNITS)
                    sp.dma_start(raw[:, u % UNITS:u % UNITS + 1, :],
                                 source.rearrange("o p n -> p o n")).then_inc(raw_loaded[u % UNITS], 16)

                for u in range(UNITS, UNITS_PER_EXPERT):
                    load(0, u)
                if follows:
                    for u in range(UNITS):
                        load(1, u)
                    nxt = snap(sp, e + 1)
                    wait(sp, ("add_rows_ready", nxt))
                    sp.wait_ge(S["exp_ready"], 1)
                    sp.dma_start(slot_rec[:, :, :], slots_of[bass.ds(nxt, 1)].rearrange("o p j r -> (o p) j r")
                                 ).then_inc(S["rec_loaded"], 16)

            experts_loop(sp, expert)
            wait(sp, ("out_stored", 16 * TILES))
            for i, s in enumerate(y_added):
                sp.wait_ge(s, 16 * EXPERTS * sum(n > i for n in BLOCKS))

        @block.gpsimd
        def _(pool):
            g = nc.gpsimd
            pool.sem_inc(S["adds_over"], 1)
            made = [0]

            def const(instruction):
                made[0] += 1
                instruction.then_inc(S["consts_made"], 1)
                pool.wait_ge(S["consts_made"], made[0])

            const(g.memset(ident[:, :], 0.0))
            const(g.affine_select(out=ident[:, :], in_=ident[:, :], compare_op=ALU.not_equal, fill=1.0,
                                  base=0, pattern=[[-1, P]], channel_multiplier=1))
            const(g.memset(minus_half[:, :], -0.5))
            const(g.memset(ones_f[:, :], 1.0))
            const(g.memset(ones[:, :], 1.0))
            const(g.iota(col_plus1[:, :], pattern=[[1, P]], base=1, channel_multiplier=0,
                         allow_small_or_imprecise_dtypes=True))
            const(g.iota(diff[:, :], pattern=[[1, P]], base=0, channel_multiplier=-1,
                         allow_small_or_imprecise_dtypes=True))
            const(g.iota(steps_left[:, :], pattern=[[0, 1]], base=P - 1, channel_multiplier=-1,
                         allow_small_or_imprecise_dtypes=True))
            const(g.iota(expert_no[:, :], pattern=[[1, EXPERTS]], base=0, channel_multiplier=0,
                         allow_small_or_imprecise_dtypes=True))
            const(g.affine_select(out=before[:, :], in_=ones_f[:, :], compare_op=ALU.is_gt, fill=0.0,
                                  base=0, pattern=[[1, P]], channel_multiplier=-1))
            blocks = same_head[:, :].rearrange("p (h e) -> p h e", e=HD)
            const(g.affine_select(out=blocks, in_=ones_f[:, :].rearrange("p (h e) -> p h e", e=HD),
                                  compare_op=ALU.is_ge, fill=0.0, base=0, pattern=[[-HD, HPG], [0, HD]],
                                  channel_multiplier=1))
            const(g.affine_select(out=blocks, in_=blocks, compare_op=ALU.is_ge, fill=0.0, base=HD - 1,
                                  pattern=[[HD, HPG], [0, HD]], channel_multiplier=-1))
            for i in range(TOP):
                const(g.iota(record[:, i, 0:1], pattern=[[0, 1]], base=-P, channel_multiplier=1,
                             allow_small_or_imprecise_dtypes=True))
            const(g.memset(slot_rec[:, :, :], 0.0))
            for j, n in enumerate(BLOCKS):
                const(g.iota(slot_rec[:, STARTS[j]:STARTS[j] + n, 0:1].rearrange("p j o -> p (j o)"),
                             pattern=[[P, n]], base=TOKENS, channel_multiplier=1,
                             allow_small_or_imprecise_dtypes=True))
            for e in range(EXPERTS):
                pool.dma_start(slots_of[e], slot_rec[:, :, :]).then_inc(S["table_init"], 16)
            const(g.memset(y_attn[:, :], 0.0))
            for i in range(PAD_ROWS // P):
                pool.dma_start(out[TOKENS + i * P:TOKENS + (i + 1) * P, :], y_attn[:, :]).then_inc(S["pads_init"], 16)
            pool.wait_ge(S["tables_made"], HEADS)
            g.affine_select(out=intra_decay[:, :, :, :].rearrange("p r g c -> p (r g) c"),
                            in_=intra_decay[:, :, :, :].rearrange("p r g c -> p (r g) c"),
                            compare_op=ALU.is_ge, fill=0.0, base=0, pattern=[[0, HEADS], [1, P]],
                            channel_multiplier=-1).then_inc(S["tables_masked"], 1)
            pool.wait_ge(S["table_init"], 16 * EXPERTS)

            def norm_scale(n):
                wait(pool, ("var_ready", n + 1))
                g.tensor_tensor(rstd[:, :], var_eps[:, :], minus_half[:, 0:1], ALU.pow).then_inc(S["rstd_ready"], 1)

            def route(n):
                for i in range(TOP):
                    wait(pool, ("slots_ready", n + 1))
                    pool.wait_ge(S["table_init"], 16 * EXPERTS)
                    pool.indirect_dma_start(table[:, :], bass.IndirectOffsetOnAxis(ap=slot_no[:, i:i + 1], axis=0),
                                            record[:, i, :], None, bounds_check=EXPERTS * CAP - 1,
                                            oob_is_err=False).then_inc(S["routed"], 16)

            norm_scale(0)
            norm_scale(1)
            route(0)

            def tile(t, n_state, ahead, norms):
                wait(pool, ("k_ready", t + 1))
                pool.wait_ge(S["decay_made"], 1)
                g.tensor_tensor(kd[:, :].rearrange("p (h d) -> p h d", d=HD),
                                k[:, :].rearrange("p (h d) -> p h d", d=HD),
                                k_decay[:, :].unsqueeze(2).to_broadcast([P, HEADS, HD]), ALU.mult).then_inc(S["kd_ready"], 1)
                wait(pool, ("state_ready", n_state))
                g.tensor_tensor(decayed[:, :, :], state[:, :, :],
                                chunk_decay[:, :].unsqueeze(2).to_broadcast([P, GROUPS, P]), ALU.mult).then_inc(S["state_decayed"], 1)
                wait(pool, ("mean_sq_ready", t + 1))
                g.tensor_tensor(head_scale[:, :], mean_sq[:, :], minus_half[:, :], ALU.pow).then_inc(S["head_scale_ready"], 1)
                if norms:
                    norm_scale(t + 2)
                if ahead:
                    route(t + 1)

            tile.start_batch = lambda: None
            tiles_loop(pool, tile)

            def gather(e, m0, j):
                for i in range(BLOCKS[j]):
                    jt = STARTS[j] + i
                    if not (isinstance(m0, int) and m0 + jt < 2):
                        wait(pool, ("x_turned", m0 + jt - 1))
                    pool.wait_ge(S["xn_stored"], 16 * TILES)
                    pool.indirect_dma_start(xg[:, jt % 2, :], None, xn_dram[:, :],
                                            bass.IndirectOffsetOnAxis(ap=gather_row[:, jt:jt + 1], axis=0),
                                            bounds_check=TOKENS - 1, oob_is_err=False).then_inc(x_gathered[jt % 2], 16)

            def scatter(e, j):
                for i in range(BLOCKS[j]):
                    by_act = 6 * e + 2 * j + i // 2 + 1
                    by_dve = 4 * e + (0, 2, 3)[j] + i // 2 + 1
                    wait(pool, ("y_by_dve", by_dve) if i % 2 else ("y_by_act", by_act))
                    pool.wait_ge(S["pads_init"], 16 * (PAD_ROWS // P))
                    jt = STARTS[j] + i
                    pool.indirect_dma_start(out[:, :], bass.IndirectOffsetOnAxis(ap=add_row[:, jt:jt + 1], axis=0),
                                            y[:, i, :], None, compute_op=ALU.add).then_inc(y_added[i], 16)

            def confirm(e, j):
                for i in range(BLOCKS[j]):
                    uses = len(BLOCKS) * e + j + 1 if i < min(BLOCKS) else e + 1
                    wait(pool, (y_added[i], 16 * uses))
                pool.sem_inc(S["adds_over"], 1)

            pool.wait_ge(S["gather_rows_ready"], 1)
            gather(0, 0, 0)
            wait(pool, ("out_stored", 16 * TILES))

            def expert(e, follows):
                m0 = SLOT_TILES * e
                gather(e, m0, 1)
                wait(pool, ("add_rows_ready", e + 1))
                scatter(e, 0)
                gather(e, m0, 2)
                confirm(e, 0)
                scatter(e, 1)
                if follows:
                    wait(pool, ("gather_rows_ready", e + 2))
                    gather(e, m0 + SLOT_TILES, 0)
                confirm(e, 1)
                scatter(e, 2)
                confirm(e, 2)

            experts_loop(pool, expert)

        @block.scalar
        def _(act):
            a = nc.scalar
            act.sem_inc(S["y_by_act"], 1)
            act.wait_ge(S["small_loaded"], 16 * (5 + HPG))
            act.wait_ge(S["consts_made"], 9)
            a.activation(k_decay[:, :], ld_row[:, :], ACT.Exp, scale=steps_left[:, 0:1])
            a.activation(chunk_decay[:, :], ld_col[:, :], ACT.Exp, scale=float(P))
            for i in range(GROUPS):
                last = a.activation(q_decay[:, i, :], col_plus1[:, :], ACT.Exp, scale=ld_col[:, i:i + 1])
            last.then_inc(S["decay_made"], 1)
            act.wait_ge(S["dve_step"], 1)
            for h in range(HEADS):
                a.activation(intra_decay[:, h % HPG, h // HPG, :], diff[:, :], ACT.Exp,
                             scale=ld_row[:, h:h + 1]).then_inc(S["tables_made"], 1)
            a.copy(small_hi[:, :, :], small_raw[:, :, :]).then_inc(S["small_hi"], 1)
            a.copy(g2_hi[:, :], g2_raw[:, :]).then_inc(S["small_hi"], 1)

            def xnT_high(n):
                wait(act, ("xnT_made", n + 1))
                a.copy(xnT_hi[:, :, :], tp[0][:, :].rearrange("p (t c) -> p t c", t=DT)).then_inc(S["xnT_hi_made"], 1)

            xnT_high(0)
            for u in range(WEIGHT_UNITS):
                n, t = WSET[u // DT], u % DT
                act.wait_ge(raw_loaded[u % UNITS], 16 * (u // UNITS + 1))
                if n == "o" and t == 0:
                    act.wait_ge(S["dve_step"], 2)
                scale = norm_col[:, t:t + 1] if n == "o" else 1.0
                a.activation(w_hi[n][:, t, :], raw[:, u % UNITS, :], ACT.Copy, scale=scale).then_inc(S["attn_w_hi"], 1)

            def silu(n, dest, source, projected, ready):
                wait(act, (projected, n + 1))
                a.activation(dest[:, :], source[:, :], ACT.Silu).then_inc(S[ready], 1)

            def gate_high(n):
                wait(act, ("g1_projected", n + 1))
                a.copy(g1T_hi[:, :], proj[1][0:HD, 0:P]).then_inc(S["g1_hi_made"], 1)
                a.copy(logitsT[HD:, :], proj[1][HD:HD + EXPERTS, 0:P]).then_inc(S["logits_copied"], 1)

            def gate_tanh(n):
                wait(act, ("gate_projected", n + 1), ("gated_ready", n))
                a.activation(tanh_g[:, :], proj[0][:, :], ACT.Tanh, scale=0.5).then_inc(S["tanh_ready"], 1)

            silu(0, q, proj[0], "q_projected", "q_ready")
            silu(0, k, proj[1], "k_projected", "k_ready")
            silu(0, v, proj[0], "v_projected", "v_ready")
            gate_high(0)
            def turned_heads(n):
                wait(act, ("q_turned", n + 1))
                a.copy(qT[:, :, :], tp[0][:, :].rearrange("p (g c) -> p g c", g=GROUPS)).then_inc(S["qT_ready"], 1)
                wait(act, ("k_turned", n + 1))
                a.copy(kT[:, :, :], tp[1][:, :].rearrange("p (g c) -> p g c", g=GROUPS)).then_inc(S["kT_ready"], 1)

            turned_heads(0)
            gate_tanh(0)
            xnT_high(1)

            def tile(t, _, ahead, norms):
                if ahead:
                    silu(t + 1, q, proj[0], "q_projected", "q_ready")
                wait(act, ("gated_ready", t + 1))
                a.activation(squares[:, :], gated[:, :], ACT.Square).then_inc(S["squared"], 1)
                if ahead:
                    silu(t + 1, k, proj[1], "k_projected", "k_ready")
                    silu(t + 1, v, proj[0], "v_projected", "v_ready")
                    gate_high(t + 1)
                    turned_heads(t + 1)
                    gate_tanh(t + 1)
                wait(act, ("normed_turned", t + 1))
                a.copy(oT_hi[:, :, :], tp[1][:, :].rearrange("p (t c) -> p t c", t=DT)).then_inc(S["oT_hi_made"], 1)
                if norms:
                    xnT_high(t + 2)

            tile.start_batch = lambda: None
            tiles_loop(act, tile)

            def split_high(e, u):
                wait(act, (raw_loaded[u % UNITS], 16 * (WEIGHT_UNITS // UNITS + 1) + 16 * FPC * e + 16 * (u // UNITS)))
                a.copy(unit_parts(u)[0], raw[:, u % UNITS, :]).then_inc(S["ffn_hi"], 1)

            for u in range(UNITS):
                split_high(0, u)

            def turned_high(m, j, i):
                wait(act, ("x_turned", m + 1))
                a.copy(xT_hi[j][:, :, i * P:(i + 1) * P],
                       xt_bank[(STARTS[j] + i) % 2][:, :].rearrange("p (t c) -> p t c", t=DT)).then_inc(S["xT_hi_made"], 1)

            for i in range(BLOCKS[0]):
                turned_high(i, 0, i)

            def expert(e, follows):
                for j, n in enumerate(BLOCKS):
                    turn = turns(j, follows)
                    for f in range(FT):
                        wait(act, ("h_done", FT * (len(BLOCKS) * e + j) + f + 1))
                        a.activation(h_hi[f % 2][:, 0:n * P], h_bank[f % 2][:, 0:n * P], ACT.Relu).then_inc(S["h_hi_ready"], 1)
                        if f in turn:
                            i, nj = turn[f]
                            turned_high(SLOT_TILES * e + SLOT_TILES * (nj == 0) + STARTS[nj] + i, nj, i)
                        for de, u in split_units(j, f, follows):
                            split_high(e + de, u)
                        if j == 0 and f == 9:
                            wait(act, ("rec_loaded", 16 * (e + 1)), ("add_rows_ready", e))
                            a.activation(slot_exp[:, :, :], slot_rec[:, :, 1:], ACT.Exp).then_inc(S["exp_ready"], 1)
                    for i in range(0, n, 2):
                        jt = STARTS[j] + i
                        wait(act, ("y_done", len(BLOCKS) * e + j + 1), ("add_rows_ready", e + 1),
                             ("adds_over", len(BLOCKS) * e + j))
                        a.activation(y[:, i, :], y_bank[i][:, :], ACT.Copy, scale=slot_gate[:, jt:jt + 1]).then_inc(S["y_by_act"], 1)

            experts_loop(act, expert)

        @block.vector
        def _(dve):
            v_ = nc.vector
            for name in ("y_ready", "add_rows_ready", "y_by_dve"):
                dve.sem_inc(S[name], 1)
            step = Steps(dve, "dve_step")
            dve.wait_ge(S["consts_made"], 9)
            step(v_.tensor_scalar(diff[:, :], diff[:, :], 0.0, None, ALU.max))
            dve.wait_ge(S["small_loaded"], 16 * (5 + HPG))
            step(v_.tensor_scalar(norm_col[:, :], norm_col[:, :], 0.5, None, ALU.mult))
            v_.memset(taken[:, :], 0.0).then_inc(S["carry_zero"], 1)

            def norm(n, after):
                if isinstance(n, int):
                    slot = n % 4
                else:
                    slot = snap(dve, n & 3)
                wait(dve, (x_early[n], 16) if isinstance(n, int) and n < 2 else ("x_loaded", 16 * (n - 1)))
                step(v_.bn_stats(stats[:, :], x_ring[:, bass.ds(slot, 1), :].rearrange("p o d -> p (o d)")))
                step(v_.bn_aggr(moments[:, :], stats[:, :]))
                v_.tensor_scalar(var_eps[:, :], moments[:, 1:2], EPS, None, ALU.add).then_inc(S["var_ready"], 1)
                after()
                if not (isinstance(n, int) and n == 0):
                    wait(dve, ("xnT_made", n), ("xn_stored", 16 * n))
                wait(dve, ("rstd_ready", n + 1))
                v_.tensor_scalar(xn[:, :], x_ring[:, bass.ds(slot, 1), :].rearrange("p o d -> p (o d)"),
                                 moments[:, 0:1], rstd[:, 0:1], ALU.subtract, ALU.mult).then_inc(S["xn_ready"], 1)

            def xnT_low(n):
                wait(dve, ("xnT_hi_made", n + 1))
                v_.tensor_tensor(xnT_lo[:, :, :], tp[0][:, :].rearrange("p (t c) -> p t c", t=DT),
                                 xnT_hi[:, :, :].bitcast(F32), ALU.subtract).then_inc(S["xnT_lo_made"], 1)

            def gate_low(n):
                wait(dve, ("g1_hi_made", n + 1))
                v_.tensor_tensor(g1T_lo[:, :], proj[1][0:HD, 0:P], g1T_hi[:, :].bitcast(F32),
                                 ALU.subtract).then_inc(S["g1_lo_made"], 1)

            def read_logits(n):
                wait(dve, ("logits_turned", n + 1))
                v_.tensor_copy(logits[:, :], proj[1][:, P:P + EXPERTS]).then_inc(S["logits_read"], 1)

            def choose(n):
                wait(dve, ("logits_read", n + 1), ("routed", 16 * TOP * n), plain=True)
                step(v_.max(ranked[:, :], logits[:, :]))
                v_.tensor_scalar(record[:, :, 2:], logits[:, :].unsqueeze(1).to_broadcast([P, TOP, EXPERTS]),
                                 ranked[:, 0:1], None, ALU.subtract)
                v_.tensor_scalar(record[:, :, 1], ranked[:, 0:TOP], ranked[:, 0:1], None, ALU.subtract)
                v_.tensor_scalar(record[:, :, 0], record[:, :, 0], float(P), None, ALU.add)
                step(v_.max_index(rank_no[:, :], ranked[:, :], logits[:, :]))
                step(v_.tensor_copy(chosen_no[:, :], rank_no[:, 0:TOP]))
                step(v_.tensor_tensor(chosen[:, :, :], expert_no[:, :].unsqueeze(1).to_broadcast([P, TOP, EXPERTS]),
                                      chosen_no[:, :].unsqueeze(2).to_broadcast([P, TOP, EXPERTS]), ALU.is_equal))
                v_.tensor_tensor(takes[:, :], chosen[:, 0, :], chosen[:, 1, :], ALU.add).then_inc(S["takes_ready"], 1)

            def give_slots(n):
                wait(dve, ("counted", n + 1))
                dve.wait_ge(S["carry_zero"], 1)
                step(v_.tensor_tensor(place_of[:, :], tp[1][:, 0:EXPERTS], taken[:, :], ALU.add))
                v_.tensor_tensor(taken[:, :], tp[1][:, EXPERTS:2 * EXPERTS], taken[:, :], ALU.add).then_inc(S["counts_read"], 1)
                step(v_.tensor_tensor(place_sel[:, :, :], chosen[:, :, :],
                                      place_of[:, :].unsqueeze(1).to_broadcast([P, TOP, EXPERTS]), ALU.mult))
                step(v_.tensor_reduce(place[:, :], place_sel[:, :, :], AX.X, ALU.add))
                v_.tensor_scalar(over[:, :], place[:, :], float(CAP), float(DROPPED), ALU.is_ge, ALU.mult)
                step(v_.scalar_tensor_tensor(slot_f[:, :], chosen_no[:, :], float(CAP), place[:, :], ALU.mult, ALU.add))
                v_.tensor_tensor(slot_no[:, :], slot_f[:, :], over[:, :], ALU.add).then_inc(S["slots_ready"], 1)

            nothing = lambda: None
            norm(0, nothing)
            dve.wait_ge(S["small_hi"], 2)
            v_.tensor_tensor(small_lo[:, :, :], small_raw[:, :, :], small_hi[:, :, :].bitcast(F32), ALU.subtract).then_inc(S["small_lo"], 1)
            v_.tensor_tensor(g2_lo[:, :], g2_raw[:, :], g2_hi[:, :].bitcast(F32), ALU.subtract).then_inc(S["small_lo"], 1)
            xnT_low(0)
            norm(1, nothing)
            for u in range(WEIGHT_UNITS):
                n, t = WSET[u // DT], u % DT
                dve.wait_ge(S["attn_w_hi"], u + 1)
                hi = w_hi[n][:, t, :].bitcast(F32)
                if n == "o":
                    ins = v_.scalar_tensor_tensor(w_lo[n][:, t, :], raw[:, u % UNITS, :], norm_col[:, t:t + 1], hi,
                                                  ALU.mult, ALU.subtract)
                else:
                    ins = v_.tensor_tensor(w_lo[n][:, t, :], raw[:, u % UNITS, :], hi, ALU.subtract)
                ins.then_inc(S["attn_w_lo"], 1)
            gate_low(0)
            def heads_turned(n):
                wait(dve, ("qT_ready", n + 1))
                dve.wait_ge(S["decay_made"], 1)
                v_.tensor_tensor(qdT[:, :, :], tp[0][:, :].rearrange("p (g c) -> p g c", g=GROUPS), q_decay[:, :, :],
                                 ALU.mult).then_inc(S["q_decayed"], 1)

            def mask(n, rs):
                for r in rs:
                    wait(dve, ("scored", HPG * n + r + 1))
                    dve.wait_ge(S["tables_masked"], 1)
                    v_.tensor_tensor(scores[:, r, :, :], sc[r % 2][:, :].rearrange("p (g c) -> p g c", g=GROUPS),
                                     intra_decay[:, r, :, :], ALU.mult).then_inc(S["masked"], 1)

            heads_turned(0)
            read_logits(0)
            xnT_low(1)
            choose(0)
            mask(0, range(HPG))
            give_slots(0)
            prologue = step.n
            per_tile = 12

            def tile(t, n_state, ahead, norms):
                step.begin(per_tile * t + prologue if norms else prologue + per_tile * (TILES - 2) + (t - TILES + 2) * (per_tile - 2))
                wait(dve, ("attended", t + 1), ("tanh_ready", t + 1))
                v_.scalar_tensor_tensor(gated[:, :], tanh_g[:, :], 1.0, o_bank[:, :], ALU.add, ALU.mult).then_inc(S["gated_ready"], 1)
                wait(dve, ("updated", t + 1), ("state_decayed", t + 1))
                step(v_.tensor_tensor(update[:, :, :], u_bank[:, :].rearrange("p (g c) -> p g c", g=GROUPS),
                                      same_head[:, :].unsqueeze(1).to_broadcast([P, GROUPS, P]), ALU.mult))
                v_.tensor_tensor(state[:, :, :], update[:, :, :], decayed[:, :, :], ALU.add).then_inc(S["state_ready"], 1)
                wait(dve, ("squared", t + 1))
                step(v_.tensor_reduce(sum_sq[:, :], squares[:, :].rearrange("p (h d) -> p h d", d=HD), AX.X, ALU.add))
                v_.tensor_scalar(mean_sq[:, :], sum_sq[:, :], 1.0 / (4 * HD), EPS, ALU.mult, ALU.add).then_inc(S["mean_sq_ready"], 1)

                def rest():
                    if ahead:
                        gate_low(t + 1)
                    wait(dve, ("head_scale_ready", t + 1))
                    v_.tensor_tensor(normed[:, :].rearrange("p (h d) -> p h d", d=HD),
                                     gated[:, :].rearrange("p (h d) -> p h d", d=HD),
                                     head_scale[:, :].unsqueeze(2).to_broadcast([P, HEADS, HD]), ALU.mult).then_inc(S["normed_ready"], 1)

                if norms:
                    norm(t + 2, rest)
                else:
                    rest()
                if ahead:
                    heads_turned(t + 1)
                    read_logits(t + 1)
                wait(dve, ("oT_hi_made", t + 1))
                v_.tensor_tensor(oT_lo[:, :, :], tp[1][:, :].rearrange("p (t c) -> p t c", t=DT),
                                 oT_hi[:, :, :].bitcast(F32), ALU.subtract).then_inc(S["oT_lo_made"], 1)
                if norms:
                    xnT_low(t + 2)
                if ahead:
                    mask(t + 1, (0, 1))
                    choose(t + 1)
                slot = t % 4 if isinstance(t, int) else snap(dve, t & 3)
                wait(dve, ("out_projected", t + 1), ("out_stored", 16 * t))
                dve.wait_ge(S["pads_init"], 16 * (PAD_ROWS // P))
                v_.tensor_tensor(y_attn[:, :], proj[1][:, :], x_ring[:, bass.ds(slot, 1), :].rearrange("p o d -> p (o d)"),
                                 ALU.add).then_inc(S["y_ready"], 1)
                if ahead:
                    mask(t + 1, (2, 3))
                    give_slots(t + 1)
                if ahead and norms:
                    assert step.n == per_tile, step.n
                elif ahead:
                    assert step.n == per_tile - 2, step.n

            def clear_state():
                v_.memset(state[:, :, :], 0.0).then_inc(S["state_ready"], 1)

            tile.start_batch = clear_state
            tiles_loop(dve, tile)
            step.begin(step.base + step.n)

            def split_low(e, u):
                wait(dve, ("ffn_hi", UNITS_PER_EXPERT * e + u + 1))
                hi, lo = unit_parts(u)
                v_.tensor_tensor(lo, raw[:, u % UNITS, :], hi.bitcast(F32), ALU.subtract).then_inc(S["ffn_lo"], 1)

            def gather_rows(e):
                wait(dve, ("rec_loaded", 16 * (e + 1)))
                v_.tensor_scalar(gather_row[:, :], slot_rec[:, :, 0], float(TOKENS - 1), None, ALU.min).then_inc(S["gather_rows_ready"], 1)

            gather_rows(0)
            for u in range(UNITS):
                split_low(0, u)

            def turned_low(m, j, i):
                wait(dve, ("xT_hi_made", m + 1))
                part = slice(i * P, (i + 1) * P)
                v_.tensor_tensor(xT_lo[j][:, :, part], xt_bank[(STARTS[j] + i) % 2][:, :].rearrange("p (t c) -> p t c", t=DT),
                                 xT_hi[j][:, :, part].bitcast(F32), ALU.subtract).then_inc(S["xT_lo_made"], 1)

            for i in range(BLOCKS[0]):
                turned_low(i, 0, i)
            after_attention = step.base
            per_expert = 3

            def expert(e, follows):
                step.begin(per_expert * e + after_attention)
                for j, n in enumerate(BLOCKS):
                    turn = turns(j, follows)
                    for f in range(FT):
                        wait(dve, ("h_hi_ready", FT * (len(BLOCKS) * e + j) + f + 1))
                        v_.scalar_tensor_tensor(h_lo[f % 2][:, 0:n * P], h_bank[f % 2][:, 0:n * P], 0.0,
                                                h_hi[f % 2][:, 0:n * P].bitcast(F32), ALU.max, ALU.subtract).then_inc(S["h_lo_ready"], 1)
                        if f in turn:
                            i, nj = turn[f]
                            turned_low(SLOT_TILES * e + SLOT_TILES * (nj == 0) + STARTS[nj] + i, nj, i)
                        for de, u in split_units(j, f, follows):
                            split_low(e + de, u)
                        if j == 0 and f == 10:
                            wait(dve, ("exp_ready", e + 1), ("adds_over", len(BLOCKS) * e))
                            step(v_.tensor_reduce(slot_sum[:, :], slot_exp[:, :, 1:], AX.X, ALU.add))
                            step(v_.reciprocal(slot_sum[:, :], slot_sum[:, :]))
                            step(v_.tensor_tensor(slot_gate[:, :], slot_sum[:, :], slot_exp[:, :, 0], ALU.mult))
                            v_.tensor_copy(add_row[:, :], slot_rec[:, :, 0]).then_inc(S["add_rows_ready"], 1)
                        if j == 2 and f == 2 and follows:
                            wait(dve, *[(s, 16 * (SLOT_TILES // 2) * e + 16 * (SLOT_TILES // 2)) for s in x_gathered])
                            gather_rows(e + 1)
                    for i in range(1, n, 2):
                        jt = STARTS[j] + i
                        wait(dve, ("y_done", len(BLOCKS) * e + j + 1), ("adds_over", len(BLOCKS) * e + j))
                        v_.tensor_scalar(y[:, i, :], y_bank[i][:, :], slot_gate[:, jt:jt + 1], None, ALU.mult).then_inc(S["y_by_dve"], 1)
                assert step.n == per_expert

            experts_loop(dve, expert)

        @block.tensor
        def _(pe):
            mm = nc.tensor.matmul

            def product(dest, left, right, k_tiles=1, at=lambda ap, t: ap, at_r=None):
                at_r = at_r or at
                passes = [(0, 0), (0, 1), (1, 0)]
                n = k_tiles * len(passes)
                i = 0
                for t in range(k_tiles):
                    for l, r in passes:
                        last = mm(dest, at(left[l], t), at_r(right[r], t), start=(i == 0), stop=(i == n - 1))
                        i += 1
                return last

            def turn(dest, source, tiles):
                for t in range(tiles):
                    last = nc.tensor.transpose(dest[:, t * P:(t + 1) * P], source[:, t * P:(t + 1) * P], ident[:, :])
                return last

            slab = lambda ap, t: ap[:, t, :]
            xnT = (xnT_hi, xnT_lo)

            def project(n, name, dest, done):
                product(dest[:, :], xnT, (w_hi[name], w_lo[name]), DT, slab).then_inc(S[done], 1)

            def turn_xn(n):
                wait(pe, ("xn_ready", n + 1))
                turn(tp[0], xn, DT).then_inc(S["xnT_made"], 1)

            def project_small(n):
                product(proj[1][0:HD + EXPERTS, 0:P], (small_hi, small_lo), xnT, DT, slab).then_inc(S["g1_projected"], 1)

            def turn_logits(n):
                rows = slice(HD, HD + EXPERTS)
                nc.tensor.transpose(proj[1][:, P:P + EXPERTS], logitsT[rows, :], ident[rows, rows]).then_inc(S["logits_turned"], 1)

            def project_gate(n):
                wait(pe, ("logits_copied", n + 1), ("g1_lo_made", n + 1))
                product(proj[0][:, :], (g1T_hi, g1T_lo), (g2_hi, g2_lo), 1,
                        lambda ap, t: ap[:, :]).then_inc(S["gate_projected"], 1)

            def count(n):
                wait(pe, ("takes_ready", n + 1))
                mm(tp[1][:, 0:EXPERTS], before[:, :], takes[:, :], start=True, stop=True)
                mm(tp[1][:, EXPERTS:2 * EXPERTS], ones[:, :], takes[:, :], start=True, stop=True).then_inc(S["counted"], 1)

            def turn_heads(n):
                wait(pe, ("q_ready", n + 1))
                turn(tp[0], q, GROUPS).then_inc(S["q_turned"], 1)
                wait(pe, ("k_ready", n + 1), *([] if isinstance(n, int) and n == 0 else [("counts_read", n)]))
                turn(tp[1], k, GROUPS).then_inc(S["k_turned"], 1)

            def score(n, rs):
                for r in rs:
                    rows = slice(r * HD, (r + 1) * HD)
                    if r >= 2:
                        wait(pe, ("masked", HPG * n + r - 1))
                    for g in range(GROUPS):
                        last = mm(sc[r % 2][:, g * P:(g + 1) * P], kT[rows, g, :], qT[rows, g, :], start=True, stop=True)
                    last.then_inc(S["scored"], 1)

            pe.wait_ge(S["consts_made"], 12)
            turn_xn(0)
            pe.wait_ge(S["xnT_lo_made"], 1)
            pe.wait_ge(S["attn_w_lo"], DT)
            project(0, "q", proj[0], "q_projected")
            pe.wait_ge(S["attn_w_lo"], 2 * DT)
            project(0, "k", proj[1], "k_projected")
            pe.wait_ge(S["attn_w_lo"], 3 * DT)
            pe.wait_ge(S["q_ready"], 1)
            project(0, "v", proj[0], "v_projected")
            pe.wait_ge(S["small_lo"], 2)
            pe.wait_ge(S["k_ready"], 1)
            project_small(0)
            turn_heads(0)
            pe.wait_ge(S["v_ready"], 1)
            project_gate(0)
            turn_logits(0)
            wait(pe, ("q_decayed", 1), ("kT_ready", 1))
            turn_xn(1)
            score(0, range(HPG))
            count(0)
            pe.wait_ge(S["attn_w_lo"], WEIGHT_UNITS)
            pe.wait_ge(S["logits_read"], 1)

            def tile(t, n_state, ahead, norms):
                wait(pe, ("state_ready", n_state))
                for g in range(GROUPS):
                    last = mm(o_bank[:, g * P:(g + 1) * P], qdT[:, g, :], state[:, g, :], start=(g == 0), stop=False,
                              skip_group_check=True)
                last.then_inc(S["inter_done"], 1)
                if ahead:
                    wait(pe, ("xnT_lo_made", t + 2), ("tanh_ready", t + 1))
                    project(t + 1, "q", proj[0], "q_projected")
                wait(pe, ("v_ready", t + 1), ("masked", HPG * t + HPG))
                for h in range(HEADS):
                    last = mm(o_bank[:, h * HD:(h + 1) * HD], scores[:, h % HPG, h // HPG, :], v[:, h * HD:(h + 1) * HD],
                              start=False, stop=(h == HEADS - 1), skip_group_check=True)
                last.then_inc(S["attended"], 1)
                wait(pe, ("kd_ready", t + 1))
                for g in range(GROUPS):
                    last = mm(u_bank[:, g * P:(g + 1) * P], kd[:, g * P:(g + 1) * P], v[:, g * P:(g + 1) * P], start=True, stop=True)
                last.then_inc(S["updated"], 1)
                if ahead:
                    wait(pe, ("y_ready", t))
                    project(t + 1, "k", proj[1], "k_projected")
                    wait(pe, ("q_ready", t + 2))
                    project(t + 1, "v", proj[0], "v_projected")
                    wait(pe, ("k_ready", t + 2))
                    project_small(t + 1)
                    turn_heads(t + 1)
                    wait(pe, ("v_ready", t + 2))
                    project_gate(t + 1)
                    turn_logits(t + 1)
                    wait(pe, ("kT_ready", t + 2))
                wait(pe, ("normed_ready", t + 1))
                turn(tp[1], normed, DT).then_inc(S["normed_turned"], 1)
                if norms:
                    wait(pe, ("q_decayed", t + 2))
                    turn_xn(t + 2)
                if ahead:
                    score(t + 1, (0, 1))
                    wait(pe, ("logits_read", t + 2))
                wait(pe, ("oT_lo_made", t + 1))
                product(proj[1][:, :], (oT_hi, oT_lo), (w_hi["o"], w_lo["o"]), DT, slab).then_inc(S["out_projected"], 1)
                if ahead:
                    score(t + 1, (2, 3))
                    count(t + 1)

            tile.start_batch = lambda: None
            tiles_loop(pe, tile)

            def turn_gathered(m, uses, j, i):
                slot = (STARTS[j] + i) % 2
                wait(pe, (x_gathered[slot], 16 * uses))
                if not (isinstance(m, int) and m < 2):
                    wait(pe, ("xT_lo_made", m - 1))
                turn(xt_bank[slot], xg[:, slot, :], DT).then_inc(S["x_turned"], 1)

            for i in range(BLOCKS[0]):
                turn_gathered(i, i // 2 + 1, 0, i)

            def expert(e, follows):
                for j, n in enumerate(BLOCKS):
                    xT = (xT_hi[j], xT_lo[j])
                    turn_here = turns(j, follows)

                    def up(f):
                        if j == 0 and f % FPC == 0:
                            wait(pe, ("ffn_lo", UNITS_PER_EXPERT * e + 8 * (f // FPC + 1)))
                        c = f // FPC
                        cols = slice(f % FPC * P, (f % FPC + 1) * P)
                        product(h_bank[f % 2][:, 0:n * P], (w1_hi[c], w1_lo[c]), xT, DT,
                                lambda ap, t: ap[:, t, cols], lambda ap, t: ap[:, t, :]).then_inc(S["h_done"], 1)

                    def down(f):
                        wait(pe, ("h_lo_ready", FT * (len(BLOCKS) * e + j) + f + 1))
                        if f == 0:
                            wait(pe, ("y_by_act", 6 * e + 2 * j), ("y_by_dve", 4 * e + (0, 2, 3)[j]))
                        c = f // FPC
                        for i in range(n):
                            part = slice(i * P, (i + 1) * P)
                            for l, (hx, wx) in enumerate(((h_hi, w2_hi), (h_hi, w2_lo), (h_lo, w2_hi))):
                                last = mm(y_bank[i][:, :], hx[f % 2][:, part], wx[c][:, f % FPC, :],
                                          start=(f == 0 and l == 0), stop=(f == FT - 1 and l == 2))
                        return last

                    wait(pe, ("xT_lo_made", SLOT_TILES * e + STARTS[j] + n))
                    for f in range(FT):
                        up(f)
                        if f > 0:
                            down(f - 1)
                        if f in turn_here:
                            i, nj = turn_here[f]
                            jt = STARTS[nj] + i
                            turn_gathered(SLOT_TILES * e + SLOT_TILES * (nj == 0) + jt,
                                          SLOT_TILES // 2 * e + SLOT_TILES // 2 * (nj == 0) + jt // 2 + 1, nj, i)
                    down(FT - 1).then_inc(S["y_done"], 1)

            experts_loop(pe, expert)


_INS = ["L0_attn_x", "L0_attn_log_decay", "L0_attn_Wq", "L0_attn_Wk", "L0_attn_Wv", "L0_attn_Wo", "L0_attn_Wg1",
        "L0_attn_Wg2", "L0_attn_norm_w", "L0_ffn_Wg", "L0_ffn_w1", "L0_ffn_w2"]


def kernel(**inputs):
    import concourse.bacc as _bacc
    from concourse import mybir as _mybir
    from concourse.bass_utils import run_bass_kernel_spmd as _run

    nc = _bacc.Bacc("TRN2", target_bir_lowering=False, num_devices=1)
    arrays, args = {}, []
    for name in _INS:
        a = np.ascontiguousarray(inputs[name])
        arrays[f"in_{name}"] = a
        args.append(nc.dram_tensor(f"in_{name}", a.shape, _mybir.dt.from_np(a.dtype), kind="ExternalInput").ap())
    args.append(nc.dram_tensor("out_rows", (TOKENS + PAD_ROWS, D), F32, kind="ExternalOutput").ap())
    build(nc, *args)
    r = _run(nc, [arrays], core_ids=[0])
    return r.results[0]["out_rows"][:TOKENS].reshape(BATCH, SEQ, D)
```

```python
from contextlib import ExitStack

import concourse.bass as bass
import numpy as np
from concourse import mybir

F32 = mybir.dt.float32
F32R = mybir.dt.float32r
BF16 = mybir.dt.bfloat16
I32 = mybir.dt.int32
U32 = mybir.dt.uint32
ALU = mybir.AluOpType
ACT = mybir.ActivationFunctionType
AX = mybir.AxisListType

P = 128
BATCH, SEQ, D = 4, 1024, 512
TOKENS = BATCH * SEQ
TILES = TOKENS // P
CHUNKS = SEQ // P
DT = D // P
HEADS, HD = 16, 32
HPG = P // HD
GROUPS = HEADS // HPG
EPS = 1e-5

EXPERTS, TOP, FF = 8, 2, 2048
CAP = -(-5 * TOKENS * TOP // (4 * EXPERTS))
SLOT_TILES = CAP // P
FT = FF // P
FPC = 4
FCHUNKS = FT // FPC
BLOCKS = [4, 2, 4]
SPARE = 1
MAIN = (BLOCKS[0] + BLOCKS[2]) * P
FIRST = [0, BLOCKS[0], BLOCKS[0] + BLOCKS[1]]
COLUMN = [0, BLOCKS[0] + BLOCKS[2], BLOCKS[0]]
REC = 2 + EXPERTS
PAD_ROWS = max(BLOCKS) * P
DROPPED = 2 * EXPERTS * CAP
UNITS = 8
UNITS_PER_EXPERT = 2 * FT
WEIGHT_UNITS = 4 * DT


def build(nc, x, log_decay, wq, wk, wv, wo, wg1, wg2, norm_w, w_route, w1, w2, out):
    assert sum(BLOCKS) * P == CAP and CAP % P == 0
    xn_dram = nc.dram_tensor("xn_rows", (TOKENS, D), F32, kind="Internal").ap()
    table = nc.dram_tensor("slot_table", (EXPERTS * CAP, REC), F32, kind="Internal").ap()
    x_rows = x.rearrange("b n d -> (b n) d")
    by_expert = table.rearrange("(e s) r -> e s r", e=EXPERTS)
    main_slots = by_expert[:, 0:MAIN, :].rearrange("e (p j) r -> e p j r", p=P)
    spare_slots = by_expert[:, MAIN:, :].rearrange("e (p j) r -> e p j r", p=P)
    main_cols, spare_cols = slice(0, MAIN // P), slice(MAIN // P, SLOT_TILES)

    with ExitStack() as ctx:
        attention_only, experts_only = ExitStack(), ExitStack()

        def sb(name, shape, dt=F32, where=ctx):
            return where.enter_context(nc.sbuf_tensor(name, shape, dt))

        def sem(name):
            return ctx.enter_context(nc.semaphore(name))

        ident = sb("ident", [P, P])
        raw = sb("raw_weights", [P, UNITS, D])
        w1_hi, w1_lo, w2_hi, w2_lo = ([None] * FCHUNKS for _ in range(4))

        def ffn_chunk(c, where):
            for name, parts in (("w1_hi", w1_hi), ("w1_lo", w1_lo), ("w2_hi", w2_hi), ("w2_lo", w2_lo)):
                parts[c] = sb(f"{name}{c}", [P, FPC, D], F32R, where)

        ffn_chunk(0, ctx)
        xg = sb("gathered", [P, 2, D])
        slot_rec = sb("slot_rec", [P, SLOT_TILES, REC])
        gather_row = sb("gather_row", [P, SLOT_TILES], I32)
        add_row = sb("add_row", [P, SLOT_TILES], I32)
        slot_exp = sb("slot_exp", [P, SLOT_TILES, REC - 1])
        slot_sum = sb("slot_sum", [P, SLOT_TILES])
        slot_gate = sb("slot_gate", [P, SLOT_TILES])
        y_attn = sb("y_attn", [P, D])
        spare_used = sb("spare_used", [1, EXPERTS], I32)

        def asb(name, shape, dt=F32):
            return sb(name, shape, dt, attention_only)

        WSET = ("q", "k", "v", "o")
        w_hi, w_lo = {}, {}
        for n in WSET:
            w_hi[n], w_lo[n] = (asb(f"w{n}_{part}", [P, DT, D], F32R) for part in ("hi", "lo"))
        small_raw = asb("small_raw", [P, DT, HD + EXPERTS])
        small_hi = asb("small_hi", [P, DT, HD + EXPERTS], F32R)
        small_lo = asb("small_lo", [P, DT, HD + EXPERTS], F32R)
        logitsT = asb("logitsT", [HD + EXPERTS, P])
        g2_raw = asb("wg2_raw", [HD, D])
        g2_hi = asb("wg2_hi", [HD, D], F32R)
        g2_lo = asb("wg2_lo", [HD, D], F32R)
        norm_col = asb("norm_col", [P, DT])
        ld_row = asb("ld_row", [P, HEADS])
        ld_col = asb("ld_col", [P, GROUPS])
        steps_left = asb("steps_left", [P, 1])
        col_plus1 = asb("col_plus1", [P, P])
        diff = asb("diff", [P, P])
        intra_decay = asb("intra_decay", [P, HPG, GROUPS, P])
        q_decay = asb("q_decay", [P, GROUPS, P])
        k_decay = asb("k_decay", [P, HEADS])
        chunk_decay = asb("chunk_decay", [P, GROUPS])
        same_head = asb("same_head", [P, P])
        before = asb("before", [P, P], BF16)
        ones = asb("ones", [P, P], BF16)
        ones_f = asb("ones_f", [P, P])
        expert_no = asb("expert_no", [P, EXPERTS])
        minus_half = asb("minus_half", [P, HEADS])
        x_ring = asb("x_ring", [P, 4, D])
        stats = asb("stats", [P, 6])
        moments = asb("moments", [P, 2])
        var_eps = asb("var_eps", [P, 1])
        rstd = asb("rstd", [P, 1])
        xn = asb("xn", [P, D])
        xnT_hi = asb("xnT_hi", [P, DT, P], F32R)
        xnT_lo = asb("xnT_lo", [P, DT, P], F32R)
        q = asb("q", [P, D])
        k = asb("k", [P, D])
        v = asb("v", [P, D])
        kd = asb("kd", [P, D])
        qT = asb("qT", [P, GROUPS, P])
        qdT = asb("qdT", [P, GROUPS, P])
        kT = asb("kT", [P, GROUPS, P])
        scores = asb("scores", [P, HPG, GROUPS, P])
        state = asb("state", [P, GROUPS, P])
        decayed = asb("decayed", [P, GROUPS, P])
        update = asb("update", [P, GROUPS, P])
        g1T_hi = asb("g1T_hi", [HD, P], F32R)
        g1T_lo = asb("g1T_lo", [HD, P], F32R)
        tanh_g = asb("tanh_g", [P, D])
        gated = asb("gated", [P, D])
        squares = asb("squares", [P, D])
        sum_sq = asb("sum_sq", [P, HEADS])
        mean_sq = asb("mean_sq", [P, HEADS])
        head_scale = asb("head_scale", [P, HEADS])
        normed = asb("normed", [P, D])
        oT_hi = asb("oT_hi", [P, DT, P], F32R)
        oT_lo = asb("oT_lo", [P, DT, P], F32R)
        logits = asb("logits", [P, EXPERTS])
        ranked = asb("ranked", [P, 8])
        rank_no = asb("rank_no", [P, 8], U32)
        chosen_no = asb("chosen_no", [P, TOP])
        chosen = asb("chosen", [P, TOP, EXPERTS])
        takes = asb("takes", [P, EXPERTS], BF16)
        taken = asb("taken", [P, EXPERTS])
        place_of = asb("place_of", [P, EXPERTS])
        place_sel = asb("place_sel", [P, TOP, EXPERTS])
        place = asb("place", [P, TOP])
        over = asb("over", [P, TOP])
        slot_f = asb("slot_f", [P, TOP])
        slot_no = asb("slot_no", [P, TOP], I32)
        record = asb("record", [P, TOP, REC])
        attention_only.close()

        def esb(name, shape, dt=F32):
            return sb(name, shape, dt, experts_only)

        xT_hi = [esb(f"xT_hi{j}", [P, DT, n * P], F32R) for j, n in enumerate(BLOCKS)]
        xT_lo = [esb(f"xT_lo{j}", [P, DT, n * P], F32R) for j, n in enumerate(BLOCKS)]
        for c in range(1, FCHUNKS):
            ffn_chunk(c, experts_only)
        h_hi = [esb(f"h_hi{i}", [P, max(BLOCKS) * P], F32R) for i in range(2)]
        h_lo = [esb(f"h_lo{i}", [P, max(BLOCKS) * P], F32R) for i in range(2)]
        y = esb("y", [P, max(BLOCKS), D])
        experts_only.close()

        banks = [ctx.enter_context(nc.psum_tensor(f"bank{i}", [P, D], F32)) for i in range(8)]
        proj, tp, sc, o_bank, u_bank = banks[0:2], banks[2:4], banks[4:6], banks[6], banks[7]
        y_bank, xt_bank, h_bank = [banks[0], banks[1], banks[6], banks[7]], banks[2:4], banks[4:6]

        names = """waits_passed decays_loaded small_loaded norm_col_halved consts_made tables_made tables_masked decay_made carry_zero
            x_loaded xn_ready xn_stored xnT_made xnT_hi_made xnT_lo_made var_ready rstd_ready
            q_projected k_projected v_projected g1_projected gate_projected
            q_ready k_ready v_ready g1_hi_made g1_lo_made tanh_ready
            q_turned k_turned q_decayed qT_ready kT_ready scored masked
            kd_ready state_ready state_decayed inter_done updated attended
            gated_ready squared mean_sq_ready head_scale_ready normed_ready
            normed_turned oT_hi_made oT_lo_made out_projected y_ready out_stored
            logits_copied logits_turned logits_read takes_ready counted counts_read slots_ready routed
            attn_w_hi attn_w_lo small_hi small_lo
            table_init pads_init dve_step act_step
            rec_loaded spare_known gather_rows_ready add_rows_ready exp_ready
            x_turned xT_hi_made xT_lo_made h_done h_hi_ready h_lo_ready adds_over
            ffn_hi ffn_lo y_done y_by_act y_by_dve""".split()
        S = {n: sem(n) for n in names}
        x_early = [sem(f"x_loaded_early{i}") for i in range(2)]
        raw_loaded = [sem(f"raw_loaded{i}") for i in range(UNITS)]
        x_gathered = [sem(f"x_gathered{i}") for i in range(2)]
        y_added = [sem(f"y_added{i}") for i in range(max(BLOCKS))]

        STARTS_AT_ONE = ("y_ready", "out_stored", "add_rows_ready", "y_by_act", "y_by_dve",
                         "adds_over")

        block = ctx.enter_context(nc.Block())

        def snap(eng, v):
            return v if isinstance(v, int) else eng.snap(v)

        def wait(eng, *pairs, plain=False):
            values = [snap(eng, v + (s in STARTS_AT_ONE)) for s, v in pairs]
            for (s, _), v in zip(pairs, values):
                eng.wait_ge(S[s] if isinstance(s, str) else s, v)
            if plain or eng in (nc.sync, nc.gpsimd):
                eng.sem_inc(S["waits_passed"], 1)

        class Steps:

            def __init__(self, eng, name):
                self.eng, self.sem, self.base, self.n = eng, S[name], 0, 0

            def begin(self, base):
                self.base, self.n = base, 0

            def __call__(self, instruction):
                instruction.then_inc(self.sem, 1)
                self.n += 1
                wait(self.eng, (self.sem, self.base + self.n), plain=True)

        STEPS_BEFORE, STEPS_TILE, STEPS_AHEAD, STEPS_NORM = 3, 0, 9, 1

        def tiles_loop(eng, body):
            with eng.Fori(0, BATCH - 1) as b:
                body.start_batch()
                with eng.Fori(0, CHUNKS) as c:
                    body(b * CHUNKS + c, b * (CHUNKS + 1) + c + 1, True, True)
            body.start_batch()
            first = (BATCH - 1) * CHUNKS
            with eng.Fori(0, CHUNKS - 2) as c:
                body(c + first, c + first + BATCH, True, True)
            for t in (TILES - 2, TILES - 1):
                body(t, t + BATCH, t < TILES - 1, False)

        def experts_loop(eng, body):
            with eng.Fori(0, EXPERTS - 1) as e:
                body(e, True)
            body(EXPERTS - 1, False)

        def turns(j, follows):
            if j == 0:
                tiles = [(i, nj) for nj in (1, 2) for i in range(BLOCKS[nj])]
                return dict(zip(range(3, FT, 2), tiles))
            if j == 2 and follows:
                return dict(zip(range(4, FT, 3), [(i, 0) for i in range(BLOCKS[0])]))
            return {}

        def spare_flag(eng, e):
            wait(eng, ("spare_known", 1))
            return eng.value_load(spare_used[0:1, bass.ds(e, 1)], min_val=0, max_val=1)

        def expert_blocks(eng, e, block, skipped):
            used = spare_flag(eng, e)
            block(0)
            with eng.If(used > 0):
                block(SPARE)
            with eng.Else():
                eng.drain()
                for name, count in skipped:
                    eng.sem_inc(S[name], count)
            block(2)

        def split_units(j, f, follows):
            if j == 0 and f < 8:
                return [(0, 8 + 3 * f + i) for i in range(3)]
            if j == len(BLOCKS) - 1 and follows and 5 <= f < 13:
                return [(1, f - 5)]
            return []

        def unit_parts(u):
            c, i = u // 8, u % 8
            hi, lo = (w1_hi, w1_lo) if i < FPC else (w2_hi, w2_lo)
            return hi[c][:, i % FPC, :], lo[c][:, i % FPC, :]

        def unit_source(e, u):
            c, i = u // 8, u % 8
            if i < FPC:
                rows = w1.rearrange("e (t p) f -> (e t) p f", p=P)
                return rows[bass.ds(e * DT + i, 1), :, c * D:(c + 1) * D]
            rows = w2.rearrange("e (t p) d -> (e t) p d", p=P)
            return rows[bass.ds(e * FT + c * FPC + i % FPC, 1), :, :]

        @block.sync
        def _(sp):
            sp.sem_inc(S["out_stored"], 1)

            def first_x(t, arrived):
                sp.dma_start(x_ring[:, t, :], x_rows[t * P:(t + 1) * P, :]).then_inc(arrived, 16)

            first_x(0, x_early[0])
            sp.dma_start(ld_row[:, :], log_decay.partition_broadcast(P)).then_inc(S["decays_loaded"], 16)
            ld_groups = log_decay.rearrange("(g h) -> h g", h=HPG)
            for h in range(HPG):
                sp.dma_start(ld_col[h * HD:(h + 1) * HD, :],
                             ld_groups[h, :].partition_broadcast(HD),
                             allow_slow_non_contiguous=True).then_inc(S["decays_loaded"], 16)

            def store_xn(n):
                row = snap(sp, n * P)
                wait(sp, ("xn_ready", n + 1))
                sp.dma_start(xn_dram[bass.ds(row, P), :], xn[:, :]).then_inc(S["xn_stored"], 16)

            for u in range(WEIGHT_UNITS):
                if u == UNITS:
                    first_x(1, x_early[1])
                if u == UNITS + DT:
                    sp.dma_start(small_raw[:, :, 0:HD], wg1.rearrange("(t p) n -> p t n", p=P)).then_inc(S["small_loaded"], 16)
                    sp.dma_start(small_raw[:, :, HD:], w_route.rearrange("(t p) n -> p t n", p=P)).then_inc(S["small_loaded"], 16)
                    sp.dma_start(g2_raw[:, :], wg2).then_inc(S["small_loaded"], 16)
                    sp.dma_start(norm_col[:, :], norm_w.rearrange("(t p) -> p t", p=P),
                                 allow_slow_non_contiguous=True).then_inc(S["small_loaded"], 16)
                    first_x(2, S["x_loaded"])
                    store_xn(0)
                w = (wq, wk, wv, wo)[u // DT]
                if u >= UNITS:
                    sp.wait_ge(S["attn_w_lo"], u - UNITS + 1)
                sp.dma_start(raw[:, u % UNITS, :], w[u % DT * P:(u % DT + 1) * P, :]).then_inc(raw_loaded[u % UNITS], 16)
            for u in range(UNITS):
                sp.wait_ge(S["attn_w_lo"], WEIGHT_UNITS - UNITS + u + 1)
                sp.dma_start(raw[:, u:u + 1, :], unit_source(0, u).rearrange("o p n -> p o n")).then_inc(raw_loaded[u], 16)

            store_xn(1)

            def tile(t):
                slot, x_row = snap(sp, (t + 3) & 3), snap(sp, (t + 3) * P)
                wait(sp, ("x_loaded", 16 * t + 16))
                wait(sp, ("y_ready", t))
                sp.dma_start(x_ring[:, bass.ds(slot, 1), :],
                             x_rows[bass.ds(x_row, P), :].unsqueeze(1)).then_inc(S["x_loaded"], 16)
                store_xn(t + 2)
                row = snap(sp, t * P)
                wait(sp, ("y_ready", t + 1))
                sp.dma_start(out[bass.ds(row, P), :], y_attn[:, :]).then_inc(S["out_stored"], 16)

            with sp.Fori(0, TILES - 3) as t:
                tile(t)
            store_xn(TILES - 1)
            for t in range(TILES - 3, TILES):
                if t == TILES - 1:
                    sp.wait_ge(S["routed"], 16 * TOP * TILES)
                    sp.dma_start(slot_rec[:, main_cols, :], main_slots[0]).then_inc(S["rec_loaded"], 16)
                    sp.dma_start(slot_rec[:, spare_cols, :], spare_slots[0]).then_inc(S["rec_loaded"], 16)
                wait(sp, ("y_ready", t + 1))
                sp.dma_start(out[t * P:(t + 1) * P, :], y_attn[:, :]).then_inc(S["out_stored"], 16)

            def expert(e, follows):
                def load(de, u):
                    source = unit_source(snap(sp, e + de), u)
                    wait(sp, ("ffn_lo", UNITS_PER_EXPERT * e + UNITS_PER_EXPERT * de + u - UNITS + 1))
                    sp.wait_ge(S["attn_w_lo"], WEIGHT_UNITS)
                    sp.dma_start(raw[:, u % UNITS:u % UNITS + 1, :],
                                 source.rearrange("o p n -> p o n")).then_inc(raw_loaded[u % UNITS], 16)

                for u in range(UNITS, UNITS_PER_EXPERT):
                    load(0, u)
                if follows:
                    for u in range(UNITS):
                        load(1, u)
                    nxt = snap(sp, e + 1)
                    wait(sp, ("add_rows_ready", nxt))
                    sp.wait_ge(S["exp_ready"], 1)
                    for cols, slots in ((main_cols, main_slots), (spare_cols, spare_slots)):
                        sp.dma_start(slot_rec[:, cols, :], slots[bass.ds(nxt, 1)].rearrange("o p j r -> (o p) j r")
                                     ).then_inc(S["rec_loaded"], 16)

            experts_loop(sp, expert)
            wait(sp, ("out_stored", 16 * TILES))
            for i, s in enumerate(y_added):
                sp.wait_ge(s, 16 * EXPERTS * sum(n > i for n in BLOCKS))

        @block.gpsimd
        def _(pool):
            g = nc.gpsimd
            pool.sem_inc(S["adds_over"], 1)
            made = [0]

            def const(instruction):
                made[0] += 1
                instruction.then_inc(S["consts_made"], 1)
                pool.wait_ge(S["consts_made"], made[0])

            const(g.memset(ident[:, :], 0.0))
            const(g.affine_select(out=ident[:, :], in_=ident[:, :], compare_op=ALU.not_equal, fill=1.0,
                                  base=0, pattern=[[-1, P]], channel_multiplier=1))
            const(g.memset(minus_half[:, :], -0.5))
            const(g.memset(ones_f[:, :], 1.0))
            const(g.memset(ones[:, :], 1.0))
            const(g.iota(col_plus1[:, :], pattern=[[1, P]], base=1, channel_multiplier=0,
                         allow_small_or_imprecise_dtypes=True))
            const(g.iota(diff[:, :], pattern=[[1, P]], base=0, channel_multiplier=-1,
                         allow_small_or_imprecise_dtypes=True))
            const(g.iota(steps_left[:, :], pattern=[[0, 1]], base=P - 1, channel_multiplier=-1,
                         allow_small_or_imprecise_dtypes=True))
            const(g.iota(expert_no[:, :], pattern=[[1, EXPERTS]], base=0, channel_multiplier=0,
                         allow_small_or_imprecise_dtypes=True))
            const(g.affine_select(out=before[:, :], in_=ones_f[:, :], compare_op=ALU.is_gt, fill=0.0,
                                  base=0, pattern=[[1, P]], channel_multiplier=-1))
            blocks = same_head[:, :].rearrange("p (h e) -> p h e", e=HD)
            const(g.affine_select(out=blocks, in_=ones_f[:, :].rearrange("p (h e) -> p h e", e=HD),
                                  compare_op=ALU.is_ge, fill=0.0, base=0, pattern=[[-HD, HPG], [0, HD]],
                                  channel_multiplier=1))
            const(g.affine_select(out=blocks, in_=blocks, compare_op=ALU.is_ge, fill=0.0, base=HD - 1,
                                  pattern=[[HD, HPG], [0, HD]], channel_multiplier=-1))
            for i in range(TOP):
                const(g.iota(record[:, i, 0:1], pattern=[[0, 1]], base=-P, channel_multiplier=1,
                             allow_small_or_imprecise_dtypes=True))
            def norm_scale(n):
                wait(pool, ("var_ready", n + 1))
                g.tensor_tensor(rstd[:, :], var_eps[:, :], minus_half[:, 0:1], ALU.pow).then_inc(S["rstd_ready"], 1)

            def route(n):
                for i in range(TOP):
                    wait(pool, ("slots_ready", n + 1))
                    pool.wait_ge(S["table_init"], 2 * 16)
                    pool.indirect_dma_start(table[:, :], bass.IndirectOffsetOnAxis(ap=slot_no[:, i:i + 1], axis=0),
                                            record[:, i, :], None, bounds_check=EXPERTS * CAP - 1,
                                            oob_is_err=False).then_inc(S["routed"], 16)

            norm_scale(0)
            const(g.memset(slot_rec[:, :, :], 0.0))
            for j, n in enumerate(BLOCKS):
                const(g.iota(slot_rec[:, COLUMN[j]:COLUMN[j] + n, 0:1].rearrange("p j o -> p (j o)"),
                             pattern=[[P, n]], base=TOKENS, channel_multiplier=1,
                             allow_small_or_imprecise_dtypes=True))
            for cols, slots in ((main_cols, main_slots), (spare_cols, spare_slots)):
                unused = slot_rec[:, cols, :].rearrange("p j r -> p (j r)")
                pool.dma_start(slots.rearrange("e p j r -> p e (j r)"),
                               unused.unsqueeze(1).to_broadcast([P, EXPERTS, unused.shape[1]])).then_inc(S["table_init"], 16)
            pool.wait_ge(S["tables_made"], HEADS)
            g.affine_select(out=intra_decay[:, :, :, :].rearrange("p r g c -> p (r g) c"),
                            in_=intra_decay[:, :, :, :].rearrange("p r g c -> p (r g) c"),
                            compare_op=ALU.is_ge, fill=0.0, base=0, pattern=[[0, HEADS], [1, P]],
                            channel_multiplier=-1).then_inc(S["tables_masked"], 1)
            pool.wait_ge(S["table_init"], 2 * 16)
            norm_scale(1)
            const(g.memset(y_attn[:, :], 0.0))
            pool.dma_start(out[TOKENS:TOKENS + PAD_ROWS, :].rearrange("(i p) d -> p i d", p=P),
                           y_attn[:, :].unsqueeze(1).to_broadcast([P, PAD_ROWS // P, D])).then_inc(S["pads_init"], 16)

            def tile(t, n_state, ahead, norms):
                wait(pool, ("k_ready", t + 1))
                pool.wait_ge(S["decay_made"], 1)
                g.tensor_tensor(kd[:, :].rearrange("p (h d) -> p h d", d=HD),
                                k[:, :].rearrange("p (h d) -> p h d", d=HD),
                                k_decay[:, :].unsqueeze(2).to_broadcast([P, HEADS, HD]), ALU.mult).then_inc(S["kd_ready"], 1)
                wait(pool, ("state_ready", n_state))
                g.tensor_tensor(decayed[:, :, :], state[:, :, :],
                                chunk_decay[:, :].unsqueeze(2).to_broadcast([P, GROUPS, P]), ALU.mult).then_inc(S["state_decayed"], 1)
                route(t)
                wait(pool, ("mean_sq_ready", t + 1))
                g.tensor_tensor(head_scale[:, :], mean_sq[:, :], minus_half[:, :], ALU.pow).then_inc(S["head_scale_ready"], 1)
                if norms:
                    norm_scale(t + 2)

            tile.start_batch = lambda: None
            tiles_loop(pool, tile)

            def gather(e, m0, j):
                for i in range(BLOCKS[j]):
                    nth, col = FIRST[j] + i, COLUMN[j] + i
                    if not (isinstance(m0, int) and m0 + nth < 2):
                        wait(pool, ("x_turned", m0 + nth - 1))
                    pool.wait_ge(S["xn_stored"], 16 * TILES)
                    pool.indirect_dma_start(xg[:, nth % 2, :], None, xn_dram[:, :],
                                            bass.IndirectOffsetOnAxis(ap=gather_row[:, col:col + 1], axis=0),
                                            bounds_check=TOKENS - 1, oob_is_err=False).then_inc(x_gathered[nth % 2], 16)

            def scatter(e, j):
                for i in range(BLOCKS[j]):
                    written = SLOT_TILES // 2 * e + FIRST[j] // 2 + i // 2 + 1
                    wait(pool, ("y_by_dve" if i % 2 else "y_by_act", written))
                    pool.wait_ge(S["pads_init"], 16)
                    col = COLUMN[j] + i
                    pool.indirect_dma_start(out[:, :], bass.IndirectOffsetOnAxis(ap=add_row[:, col:col + 1], axis=0),
                                            y[:, i, :], None, compute_op=ALU.add).then_inc(y_added[i], 16)

            def confirm(e, j):
                for i in range(BLOCKS[j]):
                    uses = [sum(n > i for n in BLOCKS[:k]) for k in (j + 1, len(BLOCKS))]
                    wait(pool, (y_added[i], 16 * uses[1] * e + 16 * uses[0]))
                pool.sem_inc(S["adds_over"], 1)

            pool.wait_ge(S["gather_rows_ready"], 1)
            gather(0, 0, 0)
            wait(pool, ("out_stored", 16 * TILES))

            def expert(e, follows):
                m0 = SLOT_TILES * e
                gather(e, m0, 1)
                gather(e, m0, 2)
                wait(pool, ("add_rows_ready", e + 1))
                scatter(e, 0)
                confirm(e, 0)
                scatter(e, 1)
                confirm(e, 1)
                if follows:
                    wait(pool, ("gather_rows_ready", e + 2))
                    gather(e, m0 + SLOT_TILES, 0)
                scatter(e, 2)
                confirm(e, 2)

            experts_loop(pool, expert)

        @block.scalar
        def _(act):
            a = nc.scalar
            act.sem_inc(S["y_by_act"], 1)
            act.wait_ge(S["decays_loaded"], 16 * (1 + HPG))
            act.wait_ge(S["consts_made"], 9)
            a.activation(k_decay[:, :], ld_row[:, :], ACT.Exp, scale=steps_left[:, 0:1])
            a.activation(chunk_decay[:, :], ld_col[:, :], ACT.Exp, scale=float(P))
            for i in range(GROUPS):
                last = a.activation(q_decay[:, i, :], col_plus1[:, :], ACT.Exp, scale=ld_col[:, i:i + 1])
            last.then_inc(S["decay_made"], 1)
            def xnT_high(n):
                wait(act, ("xnT_made", n + 1))
                a.copy(xnT_hi[:, :, :], tp[0][:, :].rearrange("p (t c) -> p t c", t=DT)).then_inc(S["xnT_hi_made"], 1)

            xnT_high(0)

            def weights_high(n):
                if n == "o":
                    act.wait_ge(S["norm_col_halved"], 1)
                for t in range(DT):
                    u = WSET.index(n) * DT + t
                    act.wait_ge(raw_loaded[u % UNITS], 16 * (u // UNITS + 1))
                    scale = norm_col[:, t:t + 1] if n == "o" else 1.0
                    a.activation(w_hi[n][:, t, :], raw[:, u % UNITS, :], ACT.Copy, scale=scale).then_inc(S["attn_w_hi"], 1)

            for n in "qk":
                weights_high(n)
            act.wait_ge(S["dve_step"], 1)
            for h in range(HEADS):
                a.activation(intra_decay[:, h % HPG, h // HPG, :], diff[:, :], ACT.Exp,
                             scale=ld_row[:, h:h + 1]).then_inc(S["tables_made"], 1)
            weights_high("v")
            act.wait_ge(S["small_loaded"], 16 * 4)
            a.copy(small_hi[:, :, :], small_raw[:, :, :]).then_inc(S["small_hi"], 1)
            a.copy(g2_hi[:, :], g2_raw[:, :]).then_inc(S["small_hi"], 1)

            def silu(n, dest, source, projected, ready):
                wait(act, (projected, n + 1))
                a.activation(dest[:, :], source[:, :], ACT.Silu).then_inc(S[ready], 1)

            def gate_high(n):
                wait(act, ("g1_projected", n + 1))
                a.copy(g1T_hi[:, :], proj[1][0:HD, 0:P]).then_inc(S["g1_hi_made"], 1)
                a.copy(logitsT[HD:, :], proj[1][HD:HD + EXPERTS, 0:P]).then_inc(S["logits_copied"], 1)

            def gate_tanh(n):
                wait(act, ("gate_projected", n + 1), ("gated_ready", n))
                a.activation(tanh_g[:, :], proj[0][:, :], ACT.Tanh, scale=0.5).then_inc(S["tanh_ready"], 1)

            silu(0, q, proj[0], "q_projected", "q_ready")
            silu(0, k, proj[1], "k_projected", "k_ready")
            weights_high("o")
            silu(0, v, proj[0], "v_projected", "v_ready")
            gate_high(0)
            def turned_heads(n):
                wait(act, ("q_turned", n + 1))
                a.copy(qT[:, :, :], tp[0][:, :].rearrange("p (g c) -> p g c", g=GROUPS)).then_inc(S["qT_ready"], 1)
                wait(act, ("k_turned", n + 1))
                a.copy(kT[:, :, :], tp[1][:, :].rearrange("p (g c) -> p g c", g=GROUPS)).then_inc(S["kT_ready"], 1)

            turned_heads(0)
            gate_tanh(0)
            xnT_high(1)

            def split_high(e, u):
                wait(act, (raw_loaded[u % UNITS], 16 * (WEIGHT_UNITS // UNITS + 1) + 16 * FPC * e + 16 * (u // UNITS)))
                a.copy(unit_parts(u)[0], raw[:, u % UNITS, :]).then_inc(S["ffn_hi"], 1)

            def tile(t, _, ahead, norms):
                if ahead:
                    silu(t + 1, q, proj[0], "q_projected", "q_ready")
                wait(act, ("gated_ready", t + 1))
                a.activation(squares[:, :], gated[:, :], ACT.Square).then_inc(S["squared"], 1)
                if ahead:
                    silu(t + 1, k, proj[1], "k_projected", "k_ready")
                    silu(t + 1, v, proj[0], "v_projected", "v_ready")
                    gate_high(t + 1)
                    turned_heads(t + 1)
                    gate_tanh(t + 1)
                wait(act, ("normed_turned", t + 1))
                a.copy(oT_hi[:, :, :], tp[1][:, :].rearrange("p (t c) -> p t c", t=DT)).then_inc(S["oT_hi_made"], 1)
                if norms:
                    xnT_high(t + 2)
                elif ahead:
                    for u in range(UNITS):
                        split_high(0, u)

            tile.start_batch = lambda: None
            tiles_loop(act, tile)

            def turned_high(m, j, i):
                wait(act, ("x_turned", m + 1))
                a.copy(xT_hi[j][:, :, i * P:(i + 1) * P],
                       xt_bank[(FIRST[j] + i) % 2][:, :].rearrange("p (t c) -> p t c", t=DT)).then_inc(S["xT_hi_made"], 1)

            for i in range(BLOCKS[0]):
                turned_high(i, 0, i)

            def expert(e, follows):
                def block(j):
                    n, turn = BLOCKS[j], turns(j, follows)
                    for f in range(FT):
                        wait(act, ("h_done", FT * (len(BLOCKS) * e + j) + f + 1))
                        a.activation(h_hi[f % 2][:, 0:n * P], h_bank[f % 2][:, 0:n * P], ACT.Relu).then_inc(S["h_hi_ready"], 1)
                        if f in turn:
                            i, nj = turn[f]
                            turned_high(SLOT_TILES * e + SLOT_TILES * (nj == 0) + FIRST[nj] + i, nj, i)
                        for de, u in split_units(j, f, follows):
                            split_high(e + de, u)
                        if j == 0 and f == 9:
                            wait(act, ("rec_loaded", 32 * (e + 1)), ("add_rows_ready", e))
                            a.activation(slot_exp[:, :, :], slot_rec[:, :, 1:], ACT.Exp).then_inc(S["exp_ready"], 1)
                    for i in range(0, n, 2):
                        col = COLUMN[j] + i
                        wait(act, ("y_done", len(BLOCKS) * e + j + 1), ("add_rows_ready", e + 1),
                             ("adds_over", len(BLOCKS) * e + j))
                        a.activation(y[:, i, :], y_bank[i][:, :], ACT.Copy, scale=slot_gate[:, col:col + 1]).then_inc(S["y_by_act"], 1)

                expert_blocks(act, e, block, (("h_hi_ready", FT), ("y_by_act", BLOCKS[SPARE] // 2)))

            experts_loop(act, expert)

        @block.vector
        def _(dve):
            v_ = nc.vector
            for name in ("y_ready", "add_rows_ready", "y_by_dve"):
                dve.sem_inc(S[name], 1)
            step = Steps(dve, "dve_step")
            dve.wait_ge(S["consts_made"], 9)
            step(v_.tensor_scalar(diff[:, :], diff[:, :], 0.0, None, ALU.max))
            v_.memset(taken[:, :], 0.0).then_inc(S["carry_zero"], 1)

            def norm(n, after):
                if isinstance(n, int):
                    slot = n % 4
                else:
                    slot = snap(dve, n & 3)
                wait(dve, (x_early[n], 16) if isinstance(n, int) and n < 2 else ("x_loaded", 16 * (n - 1)))
                step(v_.bn_stats(stats[:, :], x_ring[:, bass.ds(slot, 1), :].rearrange("p o d -> p (o d)")))
                step(v_.bn_aggr(moments[:, :], stats[:, :]))
                v_.tensor_scalar(var_eps[:, :], moments[:, 1:2], EPS, None, ALU.add).then_inc(S["var_ready"], 1)
                after()
                if not (isinstance(n, int) and n == 0):
                    wait(dve, ("xnT_made", n), ("xn_stored", 16 * n))
                wait(dve, ("rstd_ready", n + 1))
                v_.tensor_scalar(xn[:, :], x_ring[:, bass.ds(slot, 1), :].rearrange("p o d -> p (o d)"),
                                 moments[:, 0:1], rstd[:, 0:1], ALU.subtract, ALU.mult).then_inc(S["xn_ready"], 1)

            def xnT_low(n):
                wait(dve, ("xnT_hi_made", n + 1))
                v_.tensor_tensor(xnT_lo[:, :, :], tp[0][:, :].rearrange("p (t c) -> p t c", t=DT),
                                 xnT_hi[:, :, :].bitcast(F32), ALU.subtract).then_inc(S["xnT_lo_made"], 1)

            def gate_low(n):
                wait(dve, ("g1_hi_made", n + 1))
                v_.tensor_tensor(g1T_lo[:, :], proj[1][0:HD, 0:P], g1T_hi[:, :].bitcast(F32),
                                 ALU.subtract).then_inc(S["g1_lo_made"], 1)

            def read_logits(n):
                wait(dve, ("logits_turned", n + 1))
                v_.tensor_copy(logits[:, :], proj[1][:, P:P + EXPERTS]).then_inc(S["logits_read"], 1)

            def choose(n):
                wait(dve, ("logits_read", n + 1), ("routed", 16 * TOP * n), plain=True)
                step(v_.max(ranked[:, :], logits[:, :]))
                v_.tensor_scalar(record[:, :, 2:], logits[:, :].unsqueeze(1).to_broadcast([P, TOP, EXPERTS]),
                                 ranked[:, 0:1], None, ALU.subtract)
                v_.tensor_scalar(record[:, :, 1], ranked[:, 0:TOP], ranked[:, 0:1], None, ALU.subtract)
                v_.tensor_scalar(record[:, :, 0], record[:, :, 0], float(P), None, ALU.add)
                step(v_.max_index(rank_no[:, :], ranked[:, :], logits[:, :]))
                step(v_.tensor_copy(chosen_no[:, :], rank_no[:, 0:TOP]))
                step(v_.tensor_tensor(chosen[:, :, :], expert_no[:, :].unsqueeze(1).to_broadcast([P, TOP, EXPERTS]),
                                      chosen_no[:, :].unsqueeze(2).to_broadcast([P, TOP, EXPERTS]), ALU.is_equal))
                v_.tensor_tensor(takes[:, :], chosen[:, 0, :], chosen[:, 1, :], ALU.add).then_inc(S["takes_ready"], 1)

            def give_slots(n):
                wait(dve, ("counted", n + 1))
                dve.wait_ge(S["carry_zero"], 1)
                step(v_.tensor_tensor(place_of[:, :], tp[1][:, 0:EXPERTS], taken[:, :], ALU.add))
                v_.tensor_tensor(taken[:, :], tp[1][:, EXPERTS:2 * EXPERTS], taken[:, :], ALU.add).then_inc(S["counts_read"], 1)
                step(v_.tensor_tensor(place_sel[:, :, :], chosen[:, :, :],
                                      place_of[:, :].unsqueeze(1).to_broadcast([P, TOP, EXPERTS]), ALU.mult))
                step(v_.tensor_reduce(place[:, :], place_sel[:, :, :], AX.X, ALU.add))
                v_.tensor_scalar(over[:, :], place[:, :], float(CAP), float(DROPPED), ALU.is_ge, ALU.mult)
                step(v_.scalar_tensor_tensor(slot_f[:, :], chosen_no[:, :], float(CAP), place[:, :], ALU.mult, ALU.add))
                v_.tensor_tensor(slot_no[:, :], slot_f[:, :], over[:, :], ALU.add).then_inc(S["slots_ready"], 1)

            def weights_low(n):
                for t in range(DT):
                    u = WSET.index(n) * DT + t
                    dve.wait_ge(S["attn_w_hi"], u + 1)
                    hi = w_hi[n][:, t, :].bitcast(F32)
                    if n == "o":
                        ins = v_.scalar_tensor_tensor(w_lo[n][:, t, :], raw[:, u % UNITS, :], norm_col[:, t:t + 1], hi,
                                                      ALU.mult, ALU.subtract)
                    else:
                        ins = v_.tensor_tensor(w_lo[n][:, t, :], raw[:, u % UNITS, :], hi, ALU.subtract)
                    ins.then_inc(S["attn_w_lo"], 1)

            nothing = lambda: None
            norm(0, nothing)
            xnT_low(0)
            for n in "qkv":
                weights_low(n)
            dve.wait_ge(S["small_hi"], 2)
            v_.tensor_tensor(small_lo[:, :, :], small_raw[:, :, :], small_hi[:, :, :].bitcast(F32), ALU.subtract).then_inc(S["small_lo"], 1)
            v_.tensor_tensor(g2_lo[:, :], g2_raw[:, :], g2_hi[:, :].bitcast(F32), ALU.subtract).then_inc(S["small_lo"], 1)
            v_.tensor_scalar(norm_col[:, :], norm_col[:, :], 0.5, None, ALU.mult).then_inc(S["norm_col_halved"], 1)
            norm(1, nothing)
            weights_low("o")
            gate_low(0)
            def heads_turned(n):
                wait(dve, ("qT_ready", n + 1))
                dve.wait_ge(S["decay_made"], 1)
                v_.tensor_tensor(qdT[:, :, :], tp[0][:, :].rearrange("p (g c) -> p g c", g=GROUPS), q_decay[:, :, :],
                                 ALU.mult).then_inc(S["q_decayed"], 1)

            def mask(n, rs):
                for r in rs:
                    wait(dve, ("scored", HPG * n + r + 1))
                    dve.wait_ge(S["tables_masked"], 1)
                    v_.tensor_tensor(scores[:, r, :, :], sc[r % 2][:, :].rearrange("p (g c) -> p g c", g=GROUPS),
                                     intra_decay[:, r, :, :], ALU.mult).then_inc(S["masked"], 1)

            heads_turned(0)
            read_logits(0)
            xnT_low(1)
            mask(0, (0, 1))
            choose(0)
            mask(0, (2, 3))
            prologue = step.n
            per_tile = 12

            def split_low(e, u):
                wait(dve, ("ffn_hi", UNITS_PER_EXPERT * e + u + 1))
                hi, lo = unit_parts(u)
                v_.tensor_tensor(lo, raw[:, u % UNITS, :], hi.bitcast(F32), ALU.subtract).then_inc(S["ffn_lo"], 1)

            def gather_rows(e):
                wait(dve, ("rec_loaded", 32 * (e + 1)))
                v_.tensor_scalar(gather_row[:, :], slot_rec[:, :, 0], float(TOKENS - 1), None, ALU.min).then_inc(S["gather_rows_ready"], 1)

            def turned_low(m, j, i):
                wait(dve, ("xT_hi_made", m + 1))
                part = slice(i * P, (i + 1) * P)
                v_.tensor_tensor(xT_lo[j][:, :, part], xt_bank[(FIRST[j] + i) % 2][:, :].rearrange("p (t c) -> p t c", t=DT),
                                 xT_hi[j][:, :, part].bitcast(F32), ALU.subtract).then_inc(S["xT_lo_made"], 1)

            def tile(t, n_state, ahead, norms):
                step.begin(per_tile * t + prologue if norms else prologue + per_tile * (TILES - 2) + (t - TILES + 2) * (per_tile - 2))
                give_slots(t)
                if not ahead:
                    for u in range(UNITS // 2 - 1):
                        split_low(0, u)
                wait(dve, ("attended", t + 1), ("tanh_ready", t + 1))
                v_.scalar_tensor_tensor(gated[:, :], tanh_g[:, :], 1.0, o_bank[:, :], ALU.add, ALU.mult).then_inc(S["gated_ready"], 1)
                wait(dve, ("updated", t + 1), ("state_decayed", t + 1))
                step(v_.tensor_tensor(update[:, :, :], u_bank[:, :].rearrange("p (g c) -> p g c", g=GROUPS),
                                      same_head[:, :].unsqueeze(1).to_broadcast([P, GROUPS, P]), ALU.mult))
                v_.tensor_tensor(state[:, :, :], update[:, :, :], decayed[:, :, :], ALU.add).then_inc(S["state_ready"], 1)
                wait(dve, ("squared", t + 1))
                step(v_.tensor_reduce(sum_sq[:, :], squares[:, :].rearrange("p (h d) -> p h d", d=HD), AX.X, ALU.add))
                v_.tensor_scalar(mean_sq[:, :], sum_sq[:, :], 1.0 / (4 * HD), EPS, ALU.mult, ALU.add).then_inc(S["mean_sq_ready"], 1)

                if not ahead:
                    for u in range(UNITS // 2 - 1, UNITS):
                        split_low(0, u)
                    gather_rows(0)

                def rest():
                    wait(dve, ("head_scale_ready", t + 1))
                    v_.tensor_tensor(normed[:, :].rearrange("p (h d) -> p h d", d=HD),
                                     gated[:, :].rearrange("p (h d) -> p h d", d=HD),
                                     head_scale[:, :].unsqueeze(2).to_broadcast([P, HEADS, HD]), ALU.mult).then_inc(S["normed_ready"], 1)
                    if ahead:
                        gate_low(t + 1)

                if norms:
                    norm(t + 2, rest)
                else:
                    rest()
                if ahead:
                    heads_turned(t + 1)
                    read_logits(t + 1)
                wait(dve, ("oT_hi_made", t + 1))
                v_.tensor_tensor(oT_lo[:, :, :], tp[1][:, :].rearrange("p (t c) -> p t c", t=DT),
                                 oT_hi[:, :, :].bitcast(F32), ALU.subtract).then_inc(S["oT_lo_made"], 1)
                if norms:
                    xnT_low(t + 2)
                if ahead:
                    mask(t + 1, (0, 1))
                    choose(t + 1)
                if not ahead:
                    for i in range(2):
                        turned_low(i, 0, i)
                slot = t % 4 if isinstance(t, int) else snap(dve, t & 3)
                wait(dve, ("out_projected", t + 1), ("out_stored", 16 * t))
                dve.wait_ge(S["pads_init"], 16)
                v_.tensor_tensor(y_attn[:, :], proj[1][:, :], x_ring[:, bass.ds(slot, 1), :].rearrange("p o d -> p (o d)"),
                                 ALU.add).then_inc(S["y_ready"], 1)
                if ahead:
                    mask(t + 1, (2, 3))
                if ahead and norms:
                    assert step.n == per_tile, step.n
                elif ahead:
                    assert step.n == per_tile - 2, step.n

            def clear_state():
                v_.memset(state[:, :, :], 0.0).then_inc(S["state_ready"], 1)

            tile.start_batch = clear_state
            tiles_loop(dve, tile)
            step.begin(step.base + step.n)
            v_.tensor_scalar(spare_used[:, :], taken[0:1, :], float(MAIN), None, ALU.is_gt).then_inc(S["spare_known"], 1)

            for i in range(2, BLOCKS[0]):
                turned_low(i, 0, i)
            after_attention = step.base
            per_expert = 3

            def expert(e, follows):
                step.begin(per_expert * e + after_attention)

                def block(j):
                    n, turn = BLOCKS[j], turns(j, follows)
                    for f in range(FT):
                        wait(dve, ("h_hi_ready", FT * (len(BLOCKS) * e + j) + f + 1))
                        v_.scalar_tensor_tensor(h_lo[f % 2][:, 0:n * P], h_bank[f % 2][:, 0:n * P], 0.0,
                                                h_hi[f % 2][:, 0:n * P].bitcast(F32), ALU.max, ALU.subtract).then_inc(S["h_lo_ready"], 1)
                        if f in turn:
                            i, nj = turn[f]
                            turned_low(SLOT_TILES * e + SLOT_TILES * (nj == 0) + FIRST[nj] + i, nj, i)
                        for de, u in split_units(j, f, follows):
                            split_low(e + de, u)
                        if j == 0 and f == 10:
                            wait(dve, ("exp_ready", e + 1), ("adds_over", len(BLOCKS) * e))
                            step(v_.tensor_reduce(slot_sum[:, :], slot_exp[:, :, 1:], AX.X, ALU.add))
                            step(v_.reciprocal(slot_sum[:, :], slot_sum[:, :]))
                            step(v_.tensor_tensor(slot_gate[:, :], slot_sum[:, :], slot_exp[:, :, 0], ALU.mult))
                            v_.tensor_copy(add_row[:, :], slot_rec[:, :, 0]).then_inc(S["add_rows_ready"], 1)
                        if j == 2 and f == 0 and follows:
                            wait(dve, *[(s, 16 * (SLOT_TILES // 2) * e + 16 * (SLOT_TILES // 2)) for s in x_gathered])
                            gather_rows(e + 1)
                    for i in range(1, n, 2):
                        col = COLUMN[j] + i
                        wait(dve, ("y_done", len(BLOCKS) * e + j + 1), ("adds_over", len(BLOCKS) * e + j))
                        v_.tensor_scalar(y[:, i, :], y_bank[i][:, :], slot_gate[:, col:col + 1], None, ALU.mult).then_inc(S["y_by_dve"], 1)

                expert_blocks(dve, e, block, (("h_lo_ready", FT), ("y_by_dve", BLOCKS[SPARE] // 2)))
                assert step.n == per_expert

            experts_loop(dve, expert)

        @block.tensor
        def _(pe):
            mm = nc.tensor.matmul

            def product(dest, left, right, k_tiles=1, at=lambda ap, t: ap, at_r=None, between=lambda i: None):
                at_r = at_r or at
                passes = [(0, 0), (0, 1), (1, 0)]
                n = k_tiles * len(passes)
                i = 0
                for t in range(k_tiles):
                    for l, r in passes:
                        last = mm(dest, at(left[l], t), at_r(right[r], t), start=(i == 0), stop=(i == n - 1))
                        i += 1
                        between(i)
                return last

            def turn(dest, source, tiles):
                for t in range(tiles):
                    last = nc.tensor.transpose(dest[:, t * P:(t + 1) * P], source[:, t * P:(t + 1) * P], ident[:, :])
                return last

            slab = lambda ap, t: ap[:, t, :]
            xnT = (xnT_hi, xnT_lo)

            def project(n, name, dest, done, between=lambda i: None):
                product(dest[:, :], xnT, (w_hi[name], w_lo[name]), DT, slab, between=between).then_inc(S[done], 1)

            def turn_xn(n):
                wait(pe, ("xn_ready", n + 1))
                turn(tp[0], xn, DT).then_inc(S["xnT_made"], 1)

            def project_small(n):
                product(proj[1][0:HD + EXPERTS, 0:P], (small_hi, small_lo), xnT, DT, slab).then_inc(S["g1_projected"], 1)

            def turn_logits(n):
                rows = slice(HD, HD + EXPERTS)
                nc.tensor.transpose(proj[1][:, P:P + EXPERTS], logitsT[rows, :], ident[rows, rows]).then_inc(S["logits_turned"], 1)

            def project_gate(n):
                wait(pe, ("logits_copied", n + 1), ("g1_lo_made", n + 1))
                product(proj[0][:, :], (g1T_hi, g1T_lo), (g2_hi, g2_lo), 1,
                        lambda ap, t: ap[:, :]).then_inc(S["gate_projected"], 1)

            def count(n):
                wait(pe, ("takes_ready", n + 1))
                mm(tp[1][:, 0:EXPERTS], before[:, :], takes[:, :], start=True, stop=True)
                mm(tp[1][:, EXPERTS:2 * EXPERTS], ones[:, :], takes[:, :], start=True, stop=True).then_inc(S["counted"], 1)

            def turn_heads(n):
                wait(pe, ("q_ready", n + 1))
                turn(tp[0], q, GROUPS).then_inc(S["q_turned"], 1)
                wait(pe, ("k_ready", n + 1), *([] if isinstance(n, int) and n == 0 else [("counts_read", n)]))
                turn(tp[1], k, GROUPS).then_inc(S["k_turned"], 1)

            def score(n, rs):
                for r in rs:
                    rows = slice(r * HD, (r + 1) * HD)
                    if r >= 2:
                        wait(pe, ("masked", HPG * n + r - 1))
                    for g in range(GROUPS):
                        last = mm(sc[r % 2][:, g * P:(g + 1) * P], kT[rows, g, :], qT[rows, g, :], start=True, stop=True)
                    last.then_inc(S["scored"], 1)

            pe.wait_ge(S["consts_made"], 12)
            turn_xn(0)
            pe.wait_ge(S["xnT_lo_made"], 1)
            for name, dest, freed in (("q", proj[0], None), ("k", proj[1], None), ("v", proj[0], "q_ready")):
                first = WSET.index(name) * DT
                pe.wait_ge(S["attn_w_lo"], first + 1)
                if freed:
                    pe.wait_ge(S[freed], 1)
                project(0, name, dest, name + "_projected",
                        lambda i: i % 3 == 2 and i < 3 * DT - 1 and pe.wait_ge(S["attn_w_lo"], first + i // 3 + 2))
            pe.wait_ge(S["small_lo"], 2)
            pe.wait_ge(S["k_ready"], 1)
            project_small(0)
            turn_heads(0)
            pe.wait_ge(S["v_ready"], 1)
            project_gate(0)
            turn_logits(0)
            wait(pe, ("q_decayed", 1), ("kT_ready", 1))
            turn_xn(1)
            score(0, range(HPG))
            count(0)
            pe.wait_ge(S["attn_w_lo"], WEIGHT_UNITS)
            pe.wait_ge(S["logits_read"], 1)

            def turn_gathered(m, uses, j, i):
                slot = (FIRST[j] + i) % 2
                wait(pe, (x_gathered[slot], 16 * uses))
                if not (isinstance(m, int) and m < 2):
                    wait(pe, ("xT_lo_made", m - 1))
                turn(xt_bank[slot], xg[:, slot, :], DT).then_inc(S["x_turned"], 1)

            def tile(t, n_state, ahead, norms):
                wait(pe, ("state_ready", n_state))
                for g in range(GROUPS):
                    last = mm(o_bank[:, g * P:(g + 1) * P], qdT[:, g, :], state[:, g, :], start=(g == 0), stop=False,
                              skip_group_check=True)
                last.then_inc(S["inter_done"], 1)

                def attend(h):
                    if h == 0:
                        wait(pe, ("v_ready", t + 1), ("masked", HPG * t + HPG))
                    ins = mm(o_bank[:, h * HD:(h + 1) * HD], scores[:, h % HPG, h // HPG, :], v[:, h * HD:(h + 1) * HD],
                             start=False, stop=(h == HEADS - 1), skip_group_check=True)
                    if h == HEADS - 1:
                        ins.then_inc(S["attended"], 1)

                if ahead:
                    wait(pe, ("xnT_lo_made", t + 2), ("tanh_ready", t + 1))
                    project(t + 1, "q", proj[0], "q_projected",
                            lambda i: [attend(h) for h in range(2 * (i - 4), 2 * (i - 4) + 2) if 0 <= h < HEADS])
                else:
                    for h in range(HEADS):
                        attend(h)
                wait(pe, ("kd_ready", t + 1))
                for g in range(GROUPS):
                    last = mm(u_bank[:, g * P:(g + 1) * P], kd[:, g * P:(g + 1) * P], v[:, g * P:(g + 1) * P], start=True, stop=True)
                last.then_inc(S["updated"], 1)
                if ahead:
                    wait(pe, ("y_ready", t))
                    project(t + 1, "k", proj[1], "k_projected")
                    wait(pe, ("q_ready", t + 2))
                    project(t + 1, "v", proj[0], "v_projected")
                    wait(pe, ("k_ready", t + 2))
                    project_small(t + 1)
                    turn_heads(t + 1)
                    wait(pe, ("v_ready", t + 2))
                    project_gate(t + 1)
                    turn_logits(t + 1)
                    wait(pe, ("kT_ready", t + 2))
                wait(pe, ("normed_ready", t + 1))
                turn(tp[1], normed, DT).then_inc(S["normed_turned"], 1)
                if norms:
                    wait(pe, ("q_decayed", t + 2))
                    turn_xn(t + 2)
                if ahead:
                    score(t + 1, (0, 1))
                    wait(pe, ("logits_read", t + 2))
                if not ahead:
                    turn_gathered(0, 1, 0, 0)
                    wait(pe, ("oT_lo_made", t + 1))
                    turn_gathered(1, 1, 0, 1)
                wait(pe, ("oT_lo_made", t + 1))
                product(proj[1][:, :], (oT_hi, oT_lo), (w_hi["o"], w_lo["o"]), DT, slab).then_inc(S["out_projected"], 1)
                if ahead:
                    score(t + 1, (2, 3))
                    count(t + 1)

            tile.start_batch = lambda: None
            tiles_loop(pe, tile)

            for i in range(2, BLOCKS[0]):
                turn_gathered(i, i // 2 + 1, 0, i)

            def expert(e, follows):
                def block(j):
                    n = BLOCKS[j]
                    xT = (xT_hi[j], xT_lo[j])
                    turn_here = turns(j, follows)

                    def up(f):
                        if j == 0 and f % FPC == 0:
                            wait(pe, ("ffn_lo", UNITS_PER_EXPERT * e + 8 * (f // FPC + 1)))
                        c = f // FPC
                        cols = slice(f % FPC * P, (f % FPC + 1) * P)
                        product(h_bank[f % 2][:, 0:n * P], (w1_hi[c], w1_lo[c]), xT, DT,
                                lambda ap, t: ap[:, t, cols], lambda ap, t: ap[:, t, :]).then_inc(S["h_done"], 1)

                    def down(f):
                        wait(pe, ("h_lo_ready", FT * (len(BLOCKS) * e + j) + f + 1))
                        if f == 0:
                            wait(pe, ("y_by_act", SLOT_TILES // 2 * e + FIRST[j] // 2), ("y_by_dve", SLOT_TILES // 2 * e + FIRST[j] // 2))
                        c = f // FPC
                        for i in range(n):
                            part = slice(i * P, (i + 1) * P)
                            for l, (hx, wx) in enumerate(((h_hi, w2_hi), (h_hi, w2_lo), (h_lo, w2_hi))):
                                last = mm(y_bank[i][:, :], hx[f % 2][:, part], wx[c][:, f % FPC, :],
                                          start=(f == 0 and l == 0), stop=(f == FT - 1 and l == 2))
                        return last

                    wait(pe, ("xT_lo_made", SLOT_TILES * e + FIRST[j] + n))
                    for f in range(FT):
                        up(f)
                        if f > 0:
                            down(f - 1)
                        if f in turn_here:
                            i, nj = turn_here[f]
                            nth = FIRST[nj] + i
                            turn_gathered(SLOT_TILES * e + SLOT_TILES * (nj == 0) + nth,
                                          SLOT_TILES // 2 * e + SLOT_TILES // 2 * (nj == 0) + nth // 2 + 1, nj, i)
                    down(FT - 1).then_inc(S["y_done"], 1)

                expert_blocks(pe, e, block, (("h_done", FT), ("y_done", 1)))

            experts_loop(pe, expert)


_INS = ["L0_attn_x", "L0_attn_log_decay", "L0_attn_Wq", "L0_attn_Wk", "L0_attn_Wv", "L0_attn_Wo", "L0_attn_Wg1",
        "L0_attn_Wg2", "L0_attn_norm_w", "L0_ffn_Wg", "L0_ffn_w1", "L0_ffn_w2"]


def kernel(**inputs):
    import concourse.bacc as _bacc
    from concourse import mybir as _mybir
    from concourse.bass_utils import run_bass_kernel_spmd as _run

    nc = _bacc.Bacc("TRN2", target_bir_lowering=False, num_devices=1)
    arrays, args = {}, []
    for name in _INS:
        a = np.ascontiguousarray(inputs[name])
        arrays[f"in_{name}"] = a
        args.append(nc.dram_tensor(f"in_{name}", a.shape, _mybir.dt.from_np(a.dtype), kind="ExternalInput").ap())
    args.append(nc.dram_tensor("out_rows", (TOKENS + PAD_ROWS, D), F32, kind="ExternalOutput").ap())
    build(nc, *args)
    r = _run(nc, [arrays], core_ids=[0])
    return r.results[0]["out_rows"][:TOKENS].reshape(BATCH, SEQ, D)
```

```python
from contextlib import ExitStack

import concourse.bass as bass
import numpy as np
from concourse import mybir

F32 = mybir.dt.float32
F32R = mybir.dt.float32r
BF16 = mybir.dt.bfloat16
I32 = mybir.dt.int32
U32 = mybir.dt.uint32
ALU = mybir.AluOpType
ACT = mybir.ActivationFunctionType
AX = mybir.AxisListType

P = 128
BATCH, SEQ, D = 4, 1024, 512
TOKENS = BATCH * SEQ
TILES = TOKENS // P
CHUNKS = SEQ // P
DT = D // P
HEADS, HD = 16, 32
HPG = P // HD
GROUPS = HEADS // HPG
EPS = 1e-5

EXPERTS, TOP, FF = 8, 2, 2048
CAP = -(-5 * TOKENS * TOP // (4 * EXPERTS))
SLOT_TILES = CAP // P
FT = FF // P
FPC = 4
FCHUNKS = FT // FPC
BLOCKS = [4, 1, 1, 4]
LAST = len(BLOCKS) - 1
SPARES = LAST - 1
MAIN = (BLOCKS[0] + BLOCKS[LAST]) * P
FIRST = [sum(BLOCKS[:j]) for j in range(len(BLOCKS))]
COLUMN = [0, MAIN // P, MAIN // P + 1, BLOCKS[0]]
BY_ACT = [(n + 1) // 2 for n in BLOCKS]
BY_DVE = [n // 2 for n in BLOCKS]
REC = 2 + EXPERTS
PAD_ROWS = max(BLOCKS) * P
DROPPED = 2 * EXPERTS * CAP
UNITS = 8
UNITS_PER_EXPERT = 2 * FT
WEIGHT_UNITS = 4 * DT


def build(nc, x, log_decay, wq, wk, wv, wo, wg1, wg2, norm_w, w_route, w1, w2, out):
    assert sum(BLOCKS) * P == CAP and CAP % P == 0 and set(BLOCKS[1:LAST]) == {1}
    xn_dram = nc.dram_tensor("xn_rows", (TOKENS, D), F32, kind="Internal").ap()
    table = nc.dram_tensor("slot_table", (EXPERTS * CAP, REC), F32, kind="Internal").ap()
    x_rows = x.rearrange("b n d -> (b n) d")
    by_expert = table.rearrange("(e s) r -> e s r", e=EXPERTS)
    main_slots = by_expert[:, 0:MAIN, :].rearrange("e (p j) r -> e p j r", p=P)
    spare_slots = by_expert[:, MAIN:, :].rearrange("e (j p) r -> e p j r", p=P)
    main_cols, spare_cols = slice(0, MAIN // P), slice(MAIN // P, SLOT_TILES)

    with ExitStack() as ctx:
        attention_only, experts_only = ExitStack(), ExitStack()

        def sb(name, shape, dt=F32, where=ctx):
            return where.enter_context(nc.sbuf_tensor(name, shape, dt))

        def sem(name):
            return ctx.enter_context(nc.semaphore(name))

        ident = sb("ident", [P, P])
        raw = sb("raw_weights", [P, UNITS, D])
        w1_hi, w1_lo, w2_hi, w2_lo = ([None] * FCHUNKS for _ in range(4))

        def ffn_chunk(c, where):
            for name, parts in (("w1_hi", w1_hi), ("w1_lo", w1_lo), ("w2_hi", w2_hi), ("w2_lo", w2_lo)):
                parts[c] = sb(f"{name}{c}", [P, FPC, D], F32R, where)

        ffn_chunk(0, ctx)
        xg = sb("gathered", [P, 2, D])
        slot_rec = sb("slot_rec", [P, SLOT_TILES, REC])
        gather_row = sb("gather_row", [P, SLOT_TILES], I32)
        add_row = sb("add_row", [P, SLOT_TILES], I32)
        slot_exp = sb("slot_exp", [P, SLOT_TILES, REC - 1])
        slot_sum = sb("slot_sum", [P, SLOT_TILES])
        slot_gate = sb("slot_gate", [P, SLOT_TILES])
        y_attn = sb("y_attn", [P, D])
        spare_used = sb("spare_used", [1, SPARES, EXPERTS], I32)

        def asb(name, shape, dt=F32):
            return sb(name, shape, dt, attention_only)

        WSET = ("q", "k", "v", "o")
        w_hi, w_lo = {}, {}
        for n in WSET:
            w_hi[n], w_lo[n] = (asb(f"w{n}_{part}", [P, DT, D], F32R) for part in ("hi", "lo"))
        small_raw = asb("small_raw", [P, DT, HD + EXPERTS])
        small_hi = asb("small_hi", [P, DT, HD + EXPERTS], F32R)
        small_lo = asb("small_lo", [P, DT, HD + EXPERTS], F32R)
        logitsT = asb("logitsT", [HD + EXPERTS, P])
        g2_raw = asb("wg2_raw", [3 * HD, D])
        g2_hi = asb("wg2_hi", [3 * HD, D], F32R)
        g2_parts = asb("wg2_parts", [3 * HD, D], F32R)
        norm_col = asb("norm_col", [P, DT])
        ld_row = asb("ld_row", [P, HEADS])
        ld_col = asb("ld_col", [P, GROUPS])
        steps_left = asb("steps_left", [P, 1])
        col_plus1 = asb("col_plus1", [P, P])
        diff = asb("diff", [P, P])
        intra_decay = asb("intra_decay", [P, HPG, GROUPS, P])
        q_decay = asb("q_decay", [P, GROUPS, P])
        k_decay = asb("k_decay", [P, HEADS])
        chunk_decay = asb("chunk_decay", [P, GROUPS])
        same_head = asb("same_head", [P, P])
        before = asb("before", [P, P], BF16)
        ones = asb("ones", [P, P], BF16)
        ones_f = asb("ones_f", [P, P])
        expert_no = asb("expert_no", [P, EXPERTS])
        minus_half = asb("minus_half", [P, HEADS])
        x_ring = asb("x_ring", [P, 4, D])
        stats = asb("stats", [P, 6])
        moments = asb("moments", [P, 2])
        var_eps = asb("var_eps", [P, 1])
        rstd = asb("rstd", [P, 1])
        xn = asb("xn", [P, D])
        xnT_hi = asb("xnT_hi", [P, DT, P], F32R)
        xnT_lo = asb("xnT_lo", [P, DT, P], F32R)
        q = asb("q", [P, D])
        k = asb("k", [P, D])
        v = asb("v", [P, D])
        kd = asb("kd", [P, D])
        qT = asb("qT", [P, GROUPS, P])
        qdT = asb("qdT", [P, GROUPS, P])
        kT = asb("kT", [P, GROUPS, P])
        scores = asb("scores", [P, HPG, GROUPS, P])
        state = asb("state", [P, GROUPS, P])
        decayed = asb("decayed", [P, GROUPS, P])
        update = asb("update", [P, GROUPS, P])
        g1T_parts = asb("g1T_parts", [3 * HD, P], F32R)
        tanh_g = asb("tanh_g", [P, D])
        gated = asb("gated", [P, D])
        squares = asb("squares", [P, D])
        sum_sq = asb("sum_sq", [P, HEADS])
        mean_sq = asb("mean_sq", [P, HEADS])
        head_scale = asb("head_scale", [P, HEADS])
        normed = asb("normed", [P, D])
        oT_hi = asb("oT_hi", [P, DT, P], F32R)
        oT_lo = asb("oT_lo", [P, DT, P], F32R)
        logits = asb("logits", [P, EXPERTS])
        ranked = asb("ranked", [P, 8])
        rank_no = asb("rank_no", [P, 8], U32)
        chosen_no = asb("chosen_no", [P, TOP])
        chosen = asb("chosen", [P, TOP, EXPERTS])
        takes = asb("takes", [P, EXPERTS], BF16)
        taken = asb("taken", [P, EXPERTS])
        place_of = asb("place_of", [P, EXPERTS])
        place_sel = asb("place_sel", [P, TOP, EXPERTS])
        place = asb("place", [P, TOP])
        over = asb("over", [P, TOP])
        slot_f = asb("slot_f", [P, TOP])
        slot_no = asb("slot_no", [P, TOP], I32)
        record = asb("record", [P, TOP, REC])
        attention_only.close()

        def esb(name, shape, dt=F32):
            return sb(name, shape, dt, experts_only)

        xT_hi = [esb(f"xT_hi{j}", [P, DT, n * P], F32R) for j, n in enumerate(BLOCKS)]
        xT_lo = [esb(f"xT_lo{j}", [P, DT, n * P], F32R) for j, n in enumerate(BLOCKS)]
        for c in range(1, FCHUNKS):
            ffn_chunk(c, experts_only)
        h_hi = [esb(f"h_hi{i}", [P, max(BLOCKS) * P], F32R) for i in range(2)]
        h_lo = [esb(f"h_lo{i}", [P, max(BLOCKS) * P], F32R) for i in range(2)]
        y = esb("y", [P, max(BLOCKS), D])
        experts_only.close()

        banks = [ctx.enter_context(nc.psum_tensor(f"bank{i}", [P, D], F32)) for i in range(8)]
        proj, tp, sc, o_bank, u_bank = banks[0:2], banks[2:4], banks[4:6], banks[6], banks[7]
        y_bank, xt_bank, h_bank = [banks[0], banks[1], banks[6], banks[7]], banks[2:4], banks[4:6]

        names = """waits_passed decays_loaded small_loaded norm_col_halved consts_made tables_made tables_masked decay_made carry_zero
            x_loaded xn_ready xn_stored xnT_made xnT_hi_made xnT_lo_made var_ready rstd_ready
            q_projected k_projected v_projected g1_projected gate_projected
            q_ready k_ready v_ready g1_hi_made g1_lo_made tanh_ready
            q_turned k_turned q_decayed qT_ready kT_ready scored masked
            kd_ready state_ready state_decayed inter_done updated attended
            gated_ready squared mean_sq_ready head_scale_ready normed_ready
            normed_turned oT_hi_made oT_lo_made out_projected y_ready out_stored
            logits_copied logits_turned logits_read takes_ready counted counts_read slots_ready routed
            attn_w_hi attn_w_lo small_hi small_lo
            table_init pads_init dve_step act_step
            rec_loaded spare_known gather_rows_ready add_rows_ready exp_ready
            spare_h_done spare_h_ready spare_turned spare_hi_made spare_lo_made
            x_turned xT_hi_made xT_lo_made h_done h_hi_ready h_lo_ready adds_over
            ffn_hi ffn_lo y_done y_by_act y_by_dve""".split()
        S = {n: sem(n) for n in names}
        x_early = [sem(f"x_loaded_early{i}") for i in range(2)]
        raw_loaded = [sem(f"raw_loaded{i}") for i in range(UNITS)]
        x_gathered = [sem(f"x_gathered{i}") for i in range(2)]
        y_added = [sem(f"y_added{i}") for i in range(max(BLOCKS))]

        STARTS_AT_ONE = ("y_ready", "out_stored", "add_rows_ready", "y_by_act", "y_by_dve",
                         "adds_over", "state_ready", "inter_done")

        block = ctx.enter_context(nc.Block())

        def snap(eng, v):
            return v if isinstance(v, int) else eng.snap(v)

        def wait(eng, *pairs, plain=False):
            values = [snap(eng, v + (s in STARTS_AT_ONE)) for s, v in pairs]
            for (s, _), v in zip(pairs, values):
                eng.wait_ge(S[s] if isinstance(s, str) else s, v)
            if plain or eng in (nc.sync, nc.gpsimd):
                eng.sem_inc(S["waits_passed"], 1)

        class Steps:

            def __init__(self, eng, name):
                self.eng, self.sem, self.base, self.n = eng, S[name], 0, 0

            def begin(self, base):
                self.base, self.n = base, 0

            def __call__(self, instruction):
                instruction.then_inc(self.sem, 1)
                self.n += 1
                wait(self.eng, (self.sem, self.base + self.n), plain=True)

        def tiles_loop(eng, body):
            with eng.Fori(0, BATCH - 1) as b:
                body.start_batch(b)
                with eng.Fori(0, CHUNKS) as c:
                    body(b * CHUNKS + c, b * (CHUNKS + 1) + c + 1, True, True)
            body.start_batch(BATCH - 1)
            first = (BATCH - 1) * CHUNKS
            with eng.Fori(0, CHUNKS - 2) as c:
                body(c + first, c + first + BATCH, True, True)
            for t in (TILES - 2, TILES - 1):
                body(t, t + BATCH, t < TILES - 1, False)

        def experts_loop(eng, body):
            with eng.Fori(0, EXPERTS - 1) as e:
                body(e, True)
            body(EXPERTS - 1, False)

        def turns(j, follows):
            if j == 0:
                tiles = [(i, nj) for nj in range(1, LAST + 1) for i in range(BLOCKS[nj])]
                return dict(zip(range(3, FT, 2), tiles))
            if j == LAST and follows:
                return dict(zip(range(4, FT, 3), [(i, 0) for i in range(BLOCKS[0])]))
            return {}

        def expert_blocks(eng, e, main, spare, skipped):
            wait(eng, ("spare_known", 1))
            used = [eng.value_load(spare_used[0:1, i, bass.ds(e, 1)], min_val=0, max_val=1) for i in range(SPARES)]
            main(0)
            for i in range(SPARES):
                with eng.If(used[i] > 0):
                    spare(1 + i)
                with eng.Else():
                    eng.drain()
                    for name, count in skipped:
                        eng.sem_inc(S[name], count)
            main(LAST)

        def added_before(counts, e, j):
            return sum(counts) * e + sum(counts[:j])

        def main_count(e, j):
            return 2 * FT * e + (FT if j else 0)

        def spare_count(e, j):
            return SPARES * FCHUNKS * e + FCHUNKS * (j - 1)

        def split_units(j, f, follows):
            if j == 0 and f < 8:
                return [(0, 8 + 3 * f + i) for i in range(3)]
            if j == LAST and follows and 5 <= f < 13:
                return [(1, f - 5)]
            return []

        def unit_parts(u):
            c, i = u // 8, u % 8
            hi, lo = (w1_hi, w1_lo) if i < FPC else (w2_hi, w2_lo)
            return hi[c][:, i % FPC, :], lo[c][:, i % FPC, :]

        def unit_source(e, u):
            c, i = u // 8, u % 8
            if i < FPC:
                rows = w1.rearrange("e (t p) f -> (e t) p f", p=P)
                return rows[bass.ds(e * DT + i, 1), :, c * D:(c + 1) * D]
            rows = w2.rearrange("e (t p) d -> (e t) p d", p=P)
            return rows[bass.ds(e * FT + c * FPC + i % FPC, 1), :, :]

        @block.sync
        def _(sp):
            sp.sem_inc(S["out_stored"], 1)

            def first_x(t, arrived):
                sp.dma_start(x_ring[:, t, :], x_rows[t * P:(t + 1) * P, :]).then_inc(arrived, 16)

            first_x(0, x_early[0])
            sp.dma_start(ld_row[:, :], log_decay.partition_broadcast(P)).then_inc(S["decays_loaded"], 16)
            ld_groups = log_decay.rearrange("(g h) -> h g", h=HPG)
            for h in range(HPG):
                sp.dma_start(ld_col[h * HD:(h + 1) * HD, :],
                             ld_groups[h, :].partition_broadcast(HD),
                             allow_slow_non_contiguous=True).then_inc(S["decays_loaded"], 16)

            def store_xn(n):
                row = snap(sp, n * P)
                wait(sp, ("xn_ready", n + 1))
                sp.dma_start(xn_dram[bass.ds(row, P), :], xn[:, :]).then_inc(S["xn_stored"], 16)

            for u in range(WEIGHT_UNITS):
                if u == UNITS:
                    first_x(1, x_early[1])
                if u == UNITS + DT:
                    sp.dma_start(small_raw[:, :, 0:HD], wg1.rearrange("(t p) n -> p t n", p=P)).then_inc(S["small_loaded"], 16)
                    sp.dma_start(small_raw[:, :, HD:], w_route.rearrange("(t p) n -> p t n", p=P)).then_inc(S["small_loaded"], 16)
                    for i in range(3):
                        sp.dma_start(g2_raw[i * HD:(i + 1) * HD, :], wg2).then_inc(S["small_loaded"], 16)
                    sp.dma_start(norm_col[:, :], norm_w.rearrange("(t p) -> p t", p=P),
                                 allow_slow_non_contiguous=True).then_inc(S["small_loaded"], 16)
                    first_x(2, S["x_loaded"])
                    store_xn(0)
                w = (wq, wk, wv, wo)[u // DT]
                if u >= UNITS:
                    sp.wait_ge(S["attn_w_lo"], u - UNITS + 1)
                sp.dma_start(raw[:, u % UNITS, :], w[u % DT * P:(u % DT + 1) * P, :]).then_inc(raw_loaded[u % UNITS], 16)
            for u in range(UNITS):
                sp.wait_ge(S["attn_w_lo"], WEIGHT_UNITS - UNITS + u + 1)
                sp.dma_start(raw[:, u:u + 1, :], unit_source(0, u).rearrange("o p n -> p o n")).then_inc(raw_loaded[u], 16)

            store_xn(1)

            def tile(t):
                slot, x_row = snap(sp, (t + 3) & 3), snap(sp, (t + 3) * P)
                wait(sp, ("x_loaded", 16 * t + 16))
                wait(sp, ("y_ready", t))
                sp.dma_start(x_ring[:, bass.ds(slot, 1), :],
                             x_rows[bass.ds(x_row, P), :].unsqueeze(1)).then_inc(S["x_loaded"], 16)
                store_xn(t + 2)
                row = snap(sp, t * P)
                wait(sp, ("y_ready", t + 1))
                sp.dma_start(out[bass.ds(row, P), :], y_attn[:, :]).then_inc(S["out_stored"], 16)

            with sp.Fori(0, TILES - 3) as t:
                tile(t)
            store_xn(TILES - 1)
            for t in range(TILES - 3, TILES):
                if t == TILES - 1:
                    sp.wait_ge(S["routed"], 16 * TOP * TILES)
                    sp.dma_start(slot_rec[:, main_cols, :], main_slots[0]).then_inc(S["rec_loaded"], 16)
                    sp.dma_start(slot_rec[:, spare_cols, :], spare_slots[0]).then_inc(S["rec_loaded"], 16)
                wait(sp, ("y_ready", t + 1))
                sp.dma_start(out[t * P:(t + 1) * P, :], y_attn[:, :]).then_inc(S["out_stored"], 16)

            def expert(e, follows):
                def load(de, u):
                    source = unit_source(snap(sp, e + de), u)
                    wait(sp, ("ffn_lo", UNITS_PER_EXPERT * e + UNITS_PER_EXPERT * de + u - UNITS + 1))
                    sp.wait_ge(S["attn_w_lo"], WEIGHT_UNITS)
                    sp.dma_start(raw[:, u % UNITS:u % UNITS + 1, :],
                                 source.rearrange("o p n -> p o n")).then_inc(raw_loaded[u % UNITS], 16)

                for u in range(UNITS, UNITS_PER_EXPERT):
                    load(0, u)
                if follows:
                    for u in range(UNITS):
                        load(1, u)
                    nxt = snap(sp, e + 1)
                    wait(sp, ("add_rows_ready", nxt))
                    sp.wait_ge(S["exp_ready"], 1)
                    for cols, slots in ((main_cols, main_slots), (spare_cols, spare_slots)):
                        sp.dma_start(slot_rec[:, cols, :], slots[bass.ds(nxt, 1)].rearrange("o p j r -> (o p) j r")
                                     ).then_inc(S["rec_loaded"], 16)

            experts_loop(sp, expert)
            wait(sp, ("out_stored", 16 * TILES))
            for i, s in enumerate(y_added):
                sp.wait_ge(s, 16 * EXPERTS * sum(n > i for n in BLOCKS))

        @block.gpsimd
        def _(pool):
            g = nc.gpsimd
            pool.sem_inc(S["adds_over"], 1)
            made = [0]

            def const(instruction):
                made[0] += 1
                instruction.then_inc(S["consts_made"], 1)
                pool.wait_ge(S["consts_made"], made[0])

            const(g.memset(ident[:, :], 0.0))
            const(g.affine_select(out=ident[:, :], in_=ident[:, :], compare_op=ALU.not_equal, fill=1.0,
                                  base=0, pattern=[[-1, P]], channel_multiplier=1))
            const(g.memset(minus_half[:, :], -0.5))
            const(g.memset(ones_f[:, :], 1.0))
            const(g.memset(ones[:, :], 1.0))
            const(g.iota(col_plus1[:, :], pattern=[[1, P]], base=1, channel_multiplier=0,
                         allow_small_or_imprecise_dtypes=True))
            const(g.iota(diff[:, :], pattern=[[1, P]], base=0, channel_multiplier=-1,
                         allow_small_or_imprecise_dtypes=True))
            const(g.iota(steps_left[:, :], pattern=[[0, 1]], base=P - 1, channel_multiplier=-1,
                         allow_small_or_imprecise_dtypes=True))
            const(g.iota(expert_no[:, :], pattern=[[1, EXPERTS]], base=0, channel_multiplier=0,
                         allow_small_or_imprecise_dtypes=True))
            const(g.affine_select(out=before[:, :], in_=ones_f[:, :], compare_op=ALU.is_gt, fill=0.0,
                                  base=0, pattern=[[1, P]], channel_multiplier=-1))
            blocks = same_head[:, :].rearrange("p (h e) -> p h e", e=HD)
            const(g.affine_select(out=blocks, in_=ones_f[:, :].rearrange("p (h e) -> p h e", e=HD),
                                  compare_op=ALU.is_ge, fill=0.0, base=0, pattern=[[-HD, HPG], [0, HD]],
                                  channel_multiplier=1))
            const(g.affine_select(out=blocks, in_=blocks, compare_op=ALU.is_ge, fill=0.0, base=HD - 1,
                                  pattern=[[HD, HPG], [0, HD]], channel_multiplier=-1))
            for i in range(TOP):
                const(g.iota(record[:, i, 0:1], pattern=[[0, 1]], base=-P, channel_multiplier=1,
                             allow_small_or_imprecise_dtypes=True))
            def norm_scale(n):
                wait(pool, ("var_ready", n + 1))
                g.tensor_tensor(rstd[:, :], var_eps[:, :], minus_half[:, 0:1], ALU.pow).then_inc(S["rstd_ready"], 1)

            def route(n):
                for i in range(TOP):
                    wait(pool, ("slots_ready", n + 1))
                    pool.wait_ge(S["table_init"], 16 * (1 + SPARES))
                    pool.indirect_dma_start(table[:, :], bass.IndirectOffsetOnAxis(ap=slot_no[:, i:i + 1], axis=0),
                                            record[:, i, :], None, bounds_check=EXPERTS * CAP - 1,
                                            oob_is_err=False).then_inc(S["routed"], 16)

            norm_scale(0)
            const(g.memset(slot_rec[:, :, :], 0.0))
            for j, n in enumerate(BLOCKS):
                const(g.iota(slot_rec[:, COLUMN[j]:COLUMN[j] + n, 0:1].rearrange("p j o -> p (j o)"),
                             pattern=[[P, n]], base=TOKENS, channel_multiplier=1,
                             allow_small_or_imprecise_dtypes=True))
            unused = slot_rec[:, :, :].rearrange("p j r -> p (j r)")
            parts = [(0, by_expert[:, 0:MAIN, :].rearrange("e (p j) r -> p e (j r)", p=P))]
            for i in range(SPARES):
                rows = slice(MAIN + i * P, MAIN + (i + 1) * P)
                parts.append((COLUMN[1 + i] * REC, by_expert[:, rows, :].rearrange("e p r -> p e r")))
            for first, slots in parts:
                values = unused[:, first:first + slots.shape[2]]
                pool.dma_start(slots, values.unsqueeze(1).to_broadcast([P, EXPERTS, slots.shape[2]])
                               ).then_inc(S["table_init"], 16)
            norm_scale(1)
            pool.wait_ge(S["tables_made"], HEADS)
            g.affine_select(out=intra_decay[:, :, :, :].rearrange("p r g c -> p (r g) c"),
                            in_=intra_decay[:, :, :, :].rearrange("p r g c -> p (r g) c"),
                            compare_op=ALU.is_ge, fill=0.0, base=0, pattern=[[0, HEADS], [1, P]],
                            channel_multiplier=-1).then_inc(S["tables_masked"], 1)
            pool.wait_ge(S["table_init"], 16 * (1 + SPARES))
            const(g.memset(y_attn[:, :], 0.0))
            pool.dma_start(out[TOKENS:TOKENS + PAD_ROWS, :].rearrange("(i p) d -> p i d", p=P),
                           y_attn[:, :].unsqueeze(1).to_broadcast([P, PAD_ROWS // P, D])).then_inc(S["pads_init"], 16)

            def tile(t, n_state, ahead, norms):
                wait(pool, ("k_ready", t + 1))
                pool.wait_ge(S["decay_made"], 1)
                g.tensor_tensor(kd[:, :].rearrange("p (h d) -> p h d", d=HD),
                                k[:, :].rearrange("p (h d) -> p h d", d=HD),
                                k_decay[:, :].unsqueeze(2).to_broadcast([P, HEADS, HD]), ALU.mult).then_inc(S["kd_ready"], 1)
                wait(pool, ("state_ready", n_state))
                g.tensor_tensor(decayed[:, :, :], state[:, :, :],
                                chunk_decay[:, :].unsqueeze(2).to_broadcast([P, GROUPS, P]), ALU.mult).then_inc(S["state_decayed"], 1)
                route(t)
                wait(pool, ("mean_sq_ready", t + 1))
                g.tensor_tensor(head_scale[:, :], mean_sq[:, :], minus_half[:, :], ALU.pow).then_inc(S["head_scale_ready"], 1)
                if norms:
                    norm_scale(t + 2)

            def clear_state(b):
                wait(pool, ("state_ready", b * (CHUNKS + 1)), ("inter_done", b * CHUNKS))
                g.memset(state[:, :, :], 0.0).then_inc(S["state_ready"], 1)

            tile.start_batch = clear_state
            tiles_loop(pool, tile)

            def gather(e, m0, j):
                for i in range(BLOCKS[j]):
                    nth, col = FIRST[j] + i, COLUMN[j] + i
                    if not (isinstance(m0, int) and m0 + nth < 2):
                        wait(pool, ("x_turned", m0 + nth - 1))
                    pool.wait_ge(S["xn_stored"], 16 * TILES)
                    pool.indirect_dma_start(xg[:, nth % 2, :], None, xn_dram[:, :],
                                            bass.IndirectOffsetOnAxis(ap=gather_row[:, col:col + 1], axis=0),
                                            bounds_check=TOKENS - 1, oob_is_err=False).then_inc(x_gathered[nth % 2], 16)

            def scatter(e, j):
                for i in range(BLOCKS[j]):
                    written = added_before(BY_DVE if i % 2 else BY_ACT, e, j) + i // 2 + 1
                    wait(pool, ("y_by_dve" if i % 2 else "y_by_act", written))
                    pool.wait_ge(S["pads_init"], 16)
                    col = COLUMN[j] + i
                    pool.indirect_dma_start(out[:, :], bass.IndirectOffsetOnAxis(ap=add_row[:, col:col + 1], axis=0),
                                            y[:, i, :], None, compute_op=ALU.add).then_inc(y_added[i], 16)

            def confirm(e, j):
                for i in range(BLOCKS[j]):
                    uses = [sum(n > i for n in BLOCKS[:k]) for k in (j + 1, len(BLOCKS))]
                    wait(pool, (y_added[i], 16 * uses[1] * e + 16 * uses[0]))
                pool.sem_inc(S["adds_over"], 1)

            pool.wait_ge(S["gather_rows_ready"], 1)
            gather(0, 0, 0)
            wait(pool, ("out_stored", 16 * TILES))

            def expert(e, follows):
                m0 = SLOT_TILES * e
                for j in range(1, LAST + 1):
                    gather(e, m0, j)
                wait(pool, ("add_rows_ready", e + 1))
                for j in range(LAST):
                    scatter(e, j)
                    confirm(e, j)
                if follows:
                    wait(pool, ("gather_rows_ready", e + 2))
                    gather(e, m0 + SLOT_TILES, 0)
                scatter(e, LAST)
                confirm(e, LAST)

            experts_loop(pool, expert)

        @block.scalar
        def _(act):
            a = nc.scalar
            act.sem_inc(S["y_by_act"], 1)
            act.wait_ge(S["decays_loaded"], 16 * (1 + HPG))
            act.wait_ge(S["consts_made"], 9)
            a.activation(k_decay[:, :], ld_row[:, :], ACT.Exp, scale=steps_left[:, 0:1])
            a.activation(chunk_decay[:, :], ld_col[:, :], ACT.Exp, scale=float(P))
            for i in range(GROUPS):
                last = a.activation(q_decay[:, i, :], col_plus1[:, :], ACT.Exp, scale=ld_col[:, i:i + 1])
            last.then_inc(S["decay_made"], 1)
            def xnT_high(n):
                wait(act, ("xnT_made", n + 1))
                a.copy(xnT_hi[:, :, :], tp[0][:, :].rearrange("p (t c) -> p t c", t=DT)).then_inc(S["xnT_hi_made"], 1)

            xnT_high(0)

            def weights_high(n):
                if n == "o":
                    act.wait_ge(S["norm_col_halved"], 1)
                for t in range(DT):
                    u = WSET.index(n) * DT + t
                    act.wait_ge(raw_loaded[u % UNITS], 16 * (u // UNITS + 1))
                    scale = norm_col[:, t:t + 1] if n == "o" else 1.0
                    a.activation(w_hi[n][:, t, :], raw[:, u % UNITS, :], ACT.Copy, scale=scale).then_inc(S["attn_w_hi"], 1)

            for n in "qk":
                weights_high(n)
            act.wait_ge(S["dve_step"], 1)
            for h in range(HEADS):
                if h == HEADS // 2:
                    weights_high("v")
                a.activation(intra_decay[:, h % HPG, h // HPG, :], diff[:, :], ACT.Exp,
                             scale=ld_row[:, h:h + 1]).then_inc(S["tables_made"], 1)
            act.wait_ge(S["small_loaded"], 16 * 6)
            a.copy(small_hi[:, :, :], small_raw[:, :, :]).then_inc(S["small_hi"], 1)
            a.copy(g2_hi[:, :], g2_raw[:, :]).then_inc(S["small_hi"], 1)

            def silu(n, dest, source, projected, ready):
                wait(act, (projected, n + 1))
                a.activation(dest[:, :], source[:, :], ACT.Silu).then_inc(S[ready], 1)

            def gate_high(n):
                wait(act, ("g1_projected", n + 1))
                a.copy(g1T_parts[0:HD, :], proj[1][0:HD, 0:P])
                a.copy(g1T_parts[HD:2 * HD, :], proj[1][0:HD, 0:P]).then_inc(S["g1_hi_made"], 1)
                a.copy(logitsT[HD:, :], proj[1][HD:HD + EXPERTS, 0:P]).then_inc(S["logits_copied"], 1)

            def gate_tanh(n):
                wait(act, ("gate_projected", n + 1), ("gated_ready", n))
                a.activation(tanh_g[:, :], proj[0][:, :], ACT.Tanh, scale=0.5).then_inc(S["tanh_ready"], 1)

            silu(0, q, proj[0], "q_projected", "q_ready")
            silu(0, k, proj[1], "k_projected", "k_ready")
            gate_high(0)
            def turned_heads(n):
                wait(act, ("q_turned", n + 1))
                a.copy(qT[:, :, :], tp[0][:, :].rearrange("p (g c) -> p g c", g=GROUPS)).then_inc(S["qT_ready"], 1)
                wait(act, ("k_turned", n + 1))
                a.copy(kT[:, :, :], tp[1][:, :].rearrange("p (g c) -> p g c", g=GROUPS)).then_inc(S["kT_ready"], 1)

            turned_heads(0)
            gate_tanh(0)
            xnT_high(1)
            silu(0, v, o_bank, "v_projected", "v_ready")
            weights_high("o")

            def split_high(e, u):
                wait(act, (raw_loaded[u % UNITS], 16 * (WEIGHT_UNITS // UNITS + 1) + 16 * FPC * e + 16 * (u // UNITS)))
                a.copy(unit_parts(u)[0], raw[:, u % UNITS, :]).then_inc(S["ffn_hi"], 1)

            def tile(t, _, ahead, norms):
                if ahead:
                    silu(t + 1, q, proj[0], "q_projected", "q_ready")
                wait(act, ("gated_ready", t + 1))
                a.activation(squares[:, :], gated[:, :], ACT.Square).then_inc(S["squared"], 1)
                if ahead:
                    silu(t + 1, k, proj[1], "k_projected", "k_ready")
                    silu(t + 1, v, proj[0], "v_projected", "v_ready")
                    turned_heads(t + 1)
                    gate_high(t + 1)
                wait(act, ("normed_turned", t + 1))
                a.copy(oT_hi[:, :, :], o_bank[:, :].rearrange("p (t c) -> p t c", t=DT)).then_inc(S["oT_hi_made"], 1)
                if ahead:
                    gate_tanh(t + 1)
                if norms:
                    xnT_high(t + 2)
                elif ahead:
                    for u in range(UNITS):
                        split_high(0, u)

            tile.start_batch = lambda b: None
            tiles_loop(act, tile)

            def turned_high(m, j, i):
                wait(act, ("x_turned", m + 1))
                a.copy(xT_hi[j][:, :, i * P:(i + 1) * P],
                       xt_bank[(FIRST[j] + i) % 2][:, :].rearrange("p (t c) -> p t c", t=DT)).then_inc(S["xT_hi_made"], 1)

            for i in range(BLOCKS[0]):
                turned_high(i, 0, i)

            def expert(e, follows):
                def rows_out(j):
                    for i in range(0, BLOCKS[j], 2):
                        col = COLUMN[j] + i
                        wait(act, ("y_done", added_before(BLOCKS, e, j) + i + 1), ("add_rows_ready", e + 1),
                             ("adds_over", len(BLOCKS) * e + j))
                        a.activation(y[:, i, :], y_bank[i][:, :], ACT.Copy, scale=slot_gate[:, col:col + 1]).then_inc(S["y_by_act"], 1)

                def main(j):
                    n, turn = BLOCKS[j], turns(j, follows)
                    for f in range(FT):
                        wait(act, ("h_done", main_count(e, j) + f + 1))
                        a.activation(h_hi[f % 2][:, 0:n * P], h_bank[f % 2][:, 0:n * P], ACT.Relu).then_inc(S["h_hi_ready"], 1)
                        if f in turn:
                            i, nj = turn[f]
                            turned_high(SLOT_TILES * e + SLOT_TILES * (nj == 0) + FIRST[nj] + i, nj, i)
                        for de, u in split_units(j, f, follows):
                            split_high(e + de, u)
                        if j == 0 and f == 9:
                            wait(act, ("rec_loaded", 32 * (e + 1)), ("add_rows_ready", e))
                            a.activation(slot_exp[:, :, :], slot_rec[:, :, 1:], ACT.Exp).then_inc(S["exp_ready"], 1)
                    rows_out(j)

                def spare(j):
                    for c in range(FCHUNKS + 1):
                        if c < FCHUNKS:
                            wait(act, ("spare_h_done", spare_count(e, j) + c + 1))
                            a.activation(xg[:, c % 2, :], h_bank[c % 2][:, :], ACT.Relu).then_inc(S["spare_h_ready"], 1)
                        if c > 0:
                            wait(act, ("spare_turned", spare_count(e, j) + c))
                            a.copy(h_hi[(c - 1) % 2][:, :], xt_bank[(c - 1) % 2][:, :]).then_inc(S["spare_hi_made"], 1)
                    rows_out(j)

                expert_blocks(act, e, main, spare, (("spare_h_ready", FCHUNKS), ("spare_hi_made", FCHUNKS), ("y_by_act", 1)))

            experts_loop(act, expert)

        @block.vector
        def _(dve):
            v_ = nc.vector
            for name in ("y_ready", "add_rows_ready", "y_by_dve", "state_ready", "inter_done"):
                dve.sem_inc(S[name], 1)
            step = Steps(dve, "dve_step")
            dve.wait_ge(S["consts_made"], 9)
            step(v_.tensor_scalar(diff[:, :], diff[:, :], 0.0, None, ALU.max))
            v_.memset(taken[:, :], 0.0).then_inc(S["carry_zero"], 1)

            def norm(n, after):
                if isinstance(n, int):
                    slot = n % 4
                else:
                    slot = snap(dve, n & 3)
                wait(dve, (x_early[n], 16) if isinstance(n, int) and n < 2 else ("x_loaded", 16 * (n - 1)))
                step(v_.bn_stats(stats[:, :], x_ring[:, bass.ds(slot, 1), :].rearrange("p o d -> p (o d)")))
                step(v_.bn_aggr(moments[:, :], stats[:, :]))
                v_.tensor_scalar(var_eps[:, :], moments[:, 1:2], EPS, None, ALU.add).then_inc(S["var_ready"], 1)
                after()
                if not (isinstance(n, int) and n == 0):
                    wait(dve, ("xnT_made", n), ("xn_stored", 16 * n))
                wait(dve, ("rstd_ready", n + 1))
                v_.tensor_scalar(xn[:, :], x_ring[:, bass.ds(slot, 1), :].rearrange("p o d -> p (o d)"),
                                 moments[:, 0:1], rstd[:, 0:1], ALU.subtract, ALU.mult).then_inc(S["xn_ready"], 1)

            def xnT_low(n):
                wait(dve, ("xnT_hi_made", n + 1))
                v_.tensor_tensor(xnT_lo[:, :, :], tp[0][:, :].rearrange("p (t c) -> p t c", t=DT),
                                 xnT_hi[:, :, :].bitcast(F32), ALU.subtract).then_inc(S["xnT_lo_made"], 1)

            def gate_low(n):
                wait(dve, ("g1_hi_made", n + 1))
                v_.tensor_tensor(g1T_parts[2 * HD:, :], proj[1][0:HD, 0:P], g1T_parts[0:HD, :].bitcast(F32),
                                 ALU.subtract).then_inc(S["g1_lo_made"], 1)

            def read_logits(n):
                wait(dve, ("logits_turned", n + 1))
                v_.tensor_copy(logits[:, :], proj[1][:, P:P + EXPERTS]).then_inc(S["logits_read"], 1)

            def choose(n):
                wait(dve, ("logits_read", n + 1), ("routed", 16 * TOP * n), plain=True)
                step(v_.max(ranked[:, :], logits[:, :]))
                v_.tensor_scalar(record[:, :, 2:], logits[:, :].unsqueeze(1).to_broadcast([P, TOP, EXPERTS]),
                                 ranked[:, 0:1], None, ALU.subtract)
                v_.tensor_scalar(record[:, :, 1], ranked[:, 0:TOP], ranked[:, 0:1], None, ALU.subtract)
                v_.tensor_scalar(record[:, :, 0], record[:, :, 0], float(P), None, ALU.add)
                step(v_.max_index(rank_no[:, :], ranked[:, :], logits[:, :]))
                step(v_.tensor_copy(chosen_no[:, :], rank_no[:, 0:TOP]))
                step(v_.tensor_tensor(chosen[:, :, :], expert_no[:, :].unsqueeze(1).to_broadcast([P, TOP, EXPERTS]),
                                      chosen_no[:, :].unsqueeze(2).to_broadcast([P, TOP, EXPERTS]), ALU.is_equal))
                v_.tensor_tensor(takes[:, :], chosen[:, 0, :], chosen[:, 1, :], ALU.add).then_inc(S["takes_ready"], 1)

            def give_slots(n):
                wait(dve, ("counted", n + 1))
                dve.wait_ge(S["carry_zero"], 1)
                step(v_.tensor_tensor(place_of[:, :], tp[1][:, 0:EXPERTS], taken[:, :], ALU.add))
                v_.tensor_tensor(taken[:, :], tp[1][:, EXPERTS:2 * EXPERTS], taken[:, :], ALU.add).then_inc(S["counts_read"], 1)
                step(v_.tensor_tensor(place_sel[:, :, :], chosen[:, :, :],
                                      place_of[:, :].unsqueeze(1).to_broadcast([P, TOP, EXPERTS]), ALU.mult))
                step(v_.tensor_reduce(place[:, :], place_sel[:, :, :], AX.X, ALU.add))
                v_.tensor_scalar(over[:, :], place[:, :], float(CAP), float(DROPPED), ALU.is_ge, ALU.mult)
                step(v_.scalar_tensor_tensor(slot_f[:, :], chosen_no[:, :], float(CAP), place[:, :], ALU.mult, ALU.add))
                v_.tensor_tensor(slot_no[:, :], slot_f[:, :], over[:, :], ALU.add).then_inc(S["slots_ready"], 1)

            def weights_low(n):
                for t in range(DT):
                    u = WSET.index(n) * DT + t
                    dve.wait_ge(S["attn_w_hi"], u + 1)
                    hi = w_hi[n][:, t, :].bitcast(F32)
                    if n == "o":
                        ins = v_.scalar_tensor_tensor(w_lo[n][:, t, :], raw[:, u % UNITS, :], norm_col[:, t:t + 1], hi,
                                                      ALU.mult, ALU.subtract)
                    else:
                        ins = v_.tensor_tensor(w_lo[n][:, t, :], raw[:, u % UNITS, :], hi, ALU.subtract)
                    ins.then_inc(S["attn_w_lo"], 1)

            nothing = lambda: None
            norm(0, nothing)
            xnT_low(0)
            for n in "qkv":
                weights_low(n)
            dve.wait_ge(S["small_hi"], 2)
            v_.tensor_tensor(small_lo[:, :, :], small_raw[:, :, :], small_hi[:, :, :].bitcast(F32), ALU.subtract).then_inc(S["small_lo"], 1)
            for i in range(3):
                rows = slice(i * HD, (i + 1) * HD)
                hi = g2_hi[rows, :].bitcast(F32)
                if i == 1:
                    ins = v_.tensor_tensor(g2_parts[rows, :], g2_raw[rows, :], hi, ALU.subtract)
                else:
                    ins = v_.tensor_copy(g2_parts[rows, :], hi)
                ins.then_inc(S["small_lo"], 1)
            v_.tensor_scalar(norm_col[:, :], norm_col[:, :], 0.5, None, ALU.mult).then_inc(S["norm_col_halved"], 1)
            norm(1, nothing)
            gate_low(0)
            def heads_turned(n):
                wait(dve, ("qT_ready", n + 1))
                dve.wait_ge(S["decay_made"], 1)
                v_.tensor_tensor(qdT[:, :, :], tp[0][:, :].rearrange("p (g c) -> p g c", g=GROUPS), q_decay[:, :, :],
                                 ALU.mult).then_inc(S["q_decayed"], 1)

            def mask(n, rs):
                for r in rs:
                    wait(dve, ("scored", HPG * n + r + 1))
                    dve.wait_ge(S["tables_masked"], 1)
                    v_.tensor_tensor(scores[:, r, :, :], sc[r % 2][:, :].rearrange("p (g c) -> p g c", g=GROUPS),
                                     intra_decay[:, r, :, :], ALU.mult).then_inc(S["masked"], 1)

            heads_turned(0)
            read_logits(0)
            xnT_low(1)
            mask(0, (0, 1))
            choose(0)
            mask(0, (2, 3))
            weights_low("o")
            prologue = step.n
            per_tile = 12

            def split_low(e, u):
                wait(dve, ("ffn_hi", UNITS_PER_EXPERT * e + u + 1))
                hi, lo = unit_parts(u)
                v_.tensor_tensor(lo, raw[:, u % UNITS, :], hi.bitcast(F32), ALU.subtract).then_inc(S["ffn_lo"], 1)

            def gather_rows(e):
                wait(dve, ("rec_loaded", 32 * (e + 1)))
                v_.tensor_scalar(gather_row[:, :], slot_rec[:, :, 0], float(TOKENS - 1), None, ALU.min).then_inc(S["gather_rows_ready"], 1)

            def turned_low(m, j, i):
                wait(dve, ("xT_hi_made", m + 1))
                part = slice(i * P, (i + 1) * P)
                v_.tensor_tensor(xT_lo[j][:, :, part], xt_bank[(FIRST[j] + i) % 2][:, :].rearrange("p (t c) -> p t c", t=DT),
                                 xT_hi[j][:, :, part].bitcast(F32), ALU.subtract).then_inc(S["xT_lo_made"], 1)

            def tile(t, n_state, ahead, norms):
                step.begin(per_tile * t + prologue if norms else prologue + per_tile * (TILES - 2) + (t - TILES + 2) * (per_tile - 2))
                give_slots(t)
                if not ahead:
                    for u in range(3):
                        split_low(0, u)
                    v_.tensor_scalar(spare_used[:, 0, :], taken[0:1, :], float(MAIN), None, ALU.is_gt)
                    v_.tensor_scalar(spare_used[:, 1, :], taken[0:1, :], float(MAIN + P), None, ALU.is_gt).then_inc(S["spare_known"], 1)
                wait(dve, ("attended", t + 1), ("tanh_ready", t + 1))
                v_.scalar_tensor_tensor(gated[:, :], tanh_g[:, :], 1.0, o_bank[:, :], ALU.add, ALU.mult).then_inc(S["gated_ready"], 1)
                wait(dve, ("updated", t + 1), ("state_decayed", t + 1))
                step(v_.tensor_tensor(update[:, :, :], u_bank[:, :].rearrange("p (g c) -> p g c", g=GROUPS),
                                      same_head[:, :].unsqueeze(1).to_broadcast([P, GROUPS, P]), ALU.mult))
                wait(dve, ("squared", t + 1))
                step(v_.tensor_reduce(sum_sq[:, :], squares[:, :].rearrange("p (h d) -> p h d", d=HD), AX.X, ALU.add))
                v_.tensor_scalar(mean_sq[:, :], sum_sq[:, :], 1.0 / (4 * HD), EPS, ALU.mult, ALU.add).then_inc(S["mean_sq_ready"], 1)
                v_.tensor_tensor(state[:, :, :], update[:, :, :], decayed[:, :, :], ALU.add).then_inc(S["state_ready"], 1)

                if not ahead:
                    for u in range(3, 6):
                        split_low(0, u)
                    gather_rows(0)

                def rest():
                    wait(dve, ("head_scale_ready", t + 1))
                    v_.tensor_tensor(normed[:, :].rearrange("p (h d) -> p h d", d=HD),
                                     gated[:, :].rearrange("p (h d) -> p h d", d=HD),
                                     head_scale[:, :].unsqueeze(2).to_broadcast([P, HEADS, HD]), ALU.mult).then_inc(S["normed_ready"], 1)
                    if not ahead:
                        for u in range(6, UNITS):
                            split_low(0, u)

                if norms:
                    norm(t + 2, rest)
                else:
                    rest()
                if ahead:
                    heads_turned(t + 1)
                    gate_low(t + 1)
                wait(dve, ("oT_hi_made", t + 1))
                v_.tensor_tensor(oT_lo[:, :, :], o_bank[:, :].rearrange("p (t c) -> p t c", t=DT),
                                 oT_hi[:, :, :].bitcast(F32), ALU.subtract).then_inc(S["oT_lo_made"], 1)
                if ahead:
                    mask(t + 1, (0,))
                    read_logits(t + 1)
                    mask(t + 1, (1,))
                    choose(t + 1)
                if norms:
                    xnT_low(t + 2)
                if not ahead:
                    for i in range(2):
                        turned_low(i, 0, i)
                slot = t % 4 if isinstance(t, int) else snap(dve, t & 3)
                wait(dve, ("out_projected", t + 1), ("out_stored", 16 * t))
                dve.wait_ge(S["pads_init"], 16)
                v_.tensor_tensor(y_attn[:, :], proj[1][:, :], x_ring[:, bass.ds(slot, 1), :].rearrange("p o d -> p (o d)"),
                                 ALU.add).then_inc(S["y_ready"], 1)
                if ahead:
                    mask(t + 1, (2, 3))
                if ahead and norms:
                    assert step.n == per_tile, step.n
                elif ahead:
                    assert step.n == per_tile - 2, step.n

            tile.start_batch = lambda b: None
            tiles_loop(dve, tile)
            step.begin(step.base + step.n)
            for i in range(2, BLOCKS[0]):
                turned_low(i, 0, i)
            after_attention = step.base
            per_expert = 3

            def expert(e, follows):
                step.begin(per_expert * e + after_attention)

                def main(j):
                    n, turn = BLOCKS[j], turns(j, follows)
                    for f in range(FT):
                        wait(dve, ("h_hi_ready", main_count(e, j) + f + 1))
                        v_.scalar_tensor_tensor(h_lo[f % 2][:, 0:n * P], h_bank[f % 2][:, 0:n * P], 0.0,
                                                h_hi[f % 2][:, 0:n * P].bitcast(F32), ALU.max, ALU.subtract).then_inc(S["h_lo_ready"], 1)
                        if f in turn:
                            i, nj = turn[f]
                            turned_low(SLOT_TILES * e + SLOT_TILES * (nj == 0) + FIRST[nj] + i, nj, i)
                        for de, u in split_units(j, f, follows):
                            split_low(e + de, u)
                        if j == 0 and f == 10:
                            wait(dve, ("exp_ready", e + 1), ("adds_over", len(BLOCKS) * e))
                            step(v_.tensor_reduce(slot_sum[:, :], slot_exp[:, :, 1:], AX.X, ALU.add))
                            step(v_.reciprocal(slot_sum[:, :], slot_sum[:, :]))
                            step(v_.tensor_tensor(slot_gate[:, :], slot_sum[:, :], slot_exp[:, :, 0], ALU.mult))
                            v_.tensor_copy(add_row[:, :], slot_rec[:, :, 0]).then_inc(S["add_rows_ready"], 1)
                        if j == LAST and f == 0 and follows:
                            wait(dve, *[(s, 16 * (SLOT_TILES // 2) * e + 16 * (SLOT_TILES // 2)) for s in x_gathered])
                            gather_rows(e + 1)
                    for i in range(1, n, 2):
                        col = COLUMN[j] + i
                        wait(dve, ("y_done", added_before(BLOCKS, e, j) + i + 1), ("adds_over", len(BLOCKS) * e + j))
                        v_.tensor_scalar(y[:, i, :], y_bank[i][:, :], slot_gate[:, col:col + 1], None, ALU.mult).then_inc(S["y_by_dve"], 1)

                def spare(j):
                    for c in range(FCHUNKS):
                        wait(dve, ("spare_hi_made", spare_count(e, j) + c + 1))
                        v_.tensor_tensor(h_lo[c % 2][:, :], xt_bank[c % 2][:, :], h_hi[c % 2][:, :].bitcast(F32),
                                         ALU.subtract).then_inc(S["spare_lo_made"], 1)

                expert_blocks(dve, e, main, spare, (("spare_lo_made", FCHUNKS),))
                assert step.n == per_expert

            experts_loop(dve, expert)

        @block.tensor
        def _(pe):
            mm = nc.tensor.matmul

            def product(dest, left, right, k_tiles=1, at=lambda ap, t: ap, at_r=None, between=lambda i: None):
                at_r = at_r or at
                passes = [(0, 0), (0, 1), (1, 0)]
                n = k_tiles * len(passes)
                i = 0
                for t in range(k_tiles):
                    for l, r in passes:
                        last = mm(dest, at(left[l], t), at_r(right[r], t), start=(i == 0), stop=(i == n - 1))
                        i += 1
                        between(i)
                return last

            def turn(dest, source, tiles):
                for t in range(tiles):
                    last = nc.tensor.transpose(dest[:, t * P:(t + 1) * P], source[:, t * P:(t + 1) * P], ident[:, :])
                return last

            slab = lambda ap, t: ap[:, t, :]
            xnT = (xnT_hi, xnT_lo)

            def project(n, name, dest, done, between=lambda i: None):
                product(dest[:, :], xnT, (w_hi[name], w_lo[name]), DT, slab, between=between).then_inc(S[done], 1)

            def turn_xn(n):
                wait(pe, ("xn_ready", n + 1))
                turn(tp[0], xn, DT).then_inc(S["xnT_made"], 1)

            def project_small(n):
                product(proj[1][0:HD + EXPERTS, 0:P], (small_hi, small_lo), xnT, DT, slab).then_inc(S["g1_projected"], 1)

            def turn_logits(n):
                rows = slice(HD, HD + EXPERTS)
                nc.tensor.transpose(proj[1][:, P:P + EXPERTS], logitsT[rows, :], ident[rows, rows]).then_inc(S["logits_turned"], 1)

            def project_gate(n):
                wait(pe, ("logits_copied", n + 1), ("g1_lo_made", n + 1))
                mm(proj[0][:, :], g1T_parts[:, :], g2_parts[:, :], start=True, stop=True).then_inc(S["gate_projected"], 1)

            def count(n):
                wait(pe, ("takes_ready", n + 1))
                mm(tp[1][:, 0:EXPERTS], before[:, :], takes[:, :], start=True, stop=True)
                mm(tp[1][:, EXPERTS:2 * EXPERTS], ones[:, :], takes[:, :], start=True, stop=True).then_inc(S["counted"], 1)

            def turn_heads(n):
                wait(pe, ("q_ready", n + 1))
                turn(tp[0], q, GROUPS).then_inc(S["q_turned"], 1)
                wait(pe, ("k_ready", n + 1), *([] if isinstance(n, int) and n == 0 else [("counts_read", n)]))
                turn(tp[1], k, GROUPS).then_inc(S["k_turned"], 1)

            def score(n, rs):
                for r in rs:
                    rows = slice(r * HD, (r + 1) * HD)
                    if r >= 2:
                        wait(pe, ("masked", HPG * n + r - 1))
                    for g in range(GROUPS):
                        last = mm(sc[r % 2][:, g * P:(g + 1) * P], kT[rows, g, :], qT[rows, g, :], start=True, stop=True)
                    last.then_inc(S["scored"], 1)

            pe.wait_ge(S["consts_made"], 12)
            turn_xn(0)
            pe.wait_ge(S["xnT_lo_made"], 1)
            for name, dest in (("q", proj[0]), ("k", proj[1]), ("v", o_bank)):
                first = WSET.index(name) * DT
                pe.wait_ge(S["attn_w_lo"], first + 1)
                project(0, name, dest, name + "_projected",
                        lambda i: i % 3 == 2 and i < 3 * DT - 1 and pe.wait_ge(S["attn_w_lo"], first + i // 3 + 2))
            pe.wait_ge(S["small_lo"], 4)
            pe.wait_ge(S["k_ready"], 1)
            project_small(0)
            turn_heads(0)
            project_gate(0)
            turn_logits(0)
            wait(pe, ("q_decayed", 1), ("kT_ready", 1))
            turn_xn(1)
            score(0, range(HPG))
            count(0)
            pe.wait_ge(S["logits_read"], 1)
            pe.wait_ge(S["v_ready"], 1)

            def turn_gathered(m, uses, j, i):
                slot = (FIRST[j] + i) % 2
                wait(pe, (x_gathered[slot], 16 * uses))
                if not (isinstance(m, int) and m < 2):
                    wait(pe, ("xT_lo_made", m - 1))
                turn(xt_bank[slot], xg[:, slot, :], DT).then_inc(S["x_turned"], 1)

            def tile(t, n_state, ahead, norms):
                def attend_before():
                    wait(pe, ("state_ready", n_state))
                    for g in range(GROUPS):
                        last = mm(o_bank[:, g * P:(g + 1) * P], qdT[:, g, :], state[:, g, :], start=(g == 0), stop=False,
                                  skip_group_check=True)
                    last.then_inc(S["inter_done"], 1)

                def attend(h):
                    if h == 0:
                        wait(pe, ("v_ready", t + 1), ("masked", HPG * t + HPG))
                    ins = mm(o_bank[:, h * HD:(h + 1) * HD], scores[:, h % HPG, h // HPG, :], v[:, h * HD:(h + 1) * HD],
                             start=False, stop=(h == HEADS - 1), skip_group_check=True)
                    if h == HEADS - 1:
                        ins.then_inc(S["attended"], 1)

                if ahead:
                    wait(pe, ("xnT_lo_made", t + 2), ("tanh_ready", t + 1))
                    project(t + 1, "q", proj[0], "q_projected",
                            lambda i: attend_before() if i == 3 else
                            [attend(h) for h in range(2 * (i - 4), 2 * (i - 4) + 2) if 0 <= h < HEADS])
                else:
                    attend_before()
                    for h in range(HEADS):
                        attend(h)
                wait(pe, ("kd_ready", t + 1))
                for g in range(GROUPS):
                    last = mm(u_bank[:, g * P:(g + 1) * P], kd[:, g * P:(g + 1) * P], v[:, g * P:(g + 1) * P], start=True, stop=True)
                last.then_inc(S["updated"], 1)
                if ahead:
                    wait(pe, ("y_ready", t))
                    project(t + 1, "k", proj[1], "k_projected")
                    wait(pe, ("q_ready", t + 2))
                    project(t + 1, "v", proj[0], "v_projected")
                    turn_heads(t + 1)
                    project_small(t + 1)
                wait(pe, ("normed_ready", t + 1))
                turn(o_bank, normed, DT).then_inc(S["normed_turned"], 1)
                if ahead:
                    wait(pe, ("kT_ready", t + 2))
                    score(t + 1, (0, 1))
                    wait(pe, ("v_ready", t + 2))
                    project_gate(t + 1)
                    turn_logits(t + 1)
                else:
                    turn_gathered(0, 1, 0, 0)
                    turn_gathered(1, 1, 0, 1)
                if norms:
                    wait(pe, ("q_decayed", t + 2))
                    turn_xn(t + 2)
                if ahead:
                    wait(pe, ("logits_read", t + 2))
                pe.wait_ge(S["attn_w_lo"], WEIGHT_UNITS)
                wait(pe, ("oT_lo_made", t + 1))
                product(proj[1][:, :], (oT_hi, oT_lo), (w_hi["o"], w_lo["o"]), DT, slab).then_inc(S["out_projected"], 1)
                if ahead:
                    score(t + 1, (2, 3))
                    count(t + 1)

            tile.start_batch = lambda b: None
            tiles_loop(pe, tile)

            for i in range(2, BLOCKS[0]):
                turn_gathered(i, i // 2 + 1, 0, i)

            def expert(e, follows):
                def banks_read(j):
                    wait(pe, ("y_by_act", added_before(BY_ACT, e, j)), ("y_by_dve", added_before(BY_DVE, e, j)))

                def main(j):
                    n = BLOCKS[j]
                    xT = (xT_hi[j], xT_lo[j])
                    turn_here = turns(j, follows)

                    def up(f):
                        if j == 0 and f % FPC == 0:
                            wait(pe, ("ffn_lo", UNITS_PER_EXPERT * e + 8 * (f // FPC + 1)))
                        c = f // FPC
                        cols = slice(f % FPC * P, (f % FPC + 1) * P)
                        product(h_bank[f % 2][:, 0:n * P], (w1_hi[c], w1_lo[c]), xT, DT,
                                lambda ap, t: ap[:, t, cols], lambda ap, t: ap[:, t, :]).then_inc(S["h_done"], 1)

                    def down(f):
                        wait(pe, ("h_lo_ready", main_count(e, j) + f + 1))
                        if f == 0:
                            banks_read(j)
                        c = f // FPC
                        for i in range(n):
                            part = slice(i * P, (i + 1) * P)
                            for l, (hx, wx) in enumerate(((h_hi, w2_hi), (h_hi, w2_lo), (h_lo, w2_hi))):
                                last = mm(y_bank[i][:, :], hx[f % 2][:, part], wx[c][:, f % FPC, :],
                                          start=(f == 0 and l == 0), stop=(f == FT - 1 and l == 2))
                            if f == FT - 1:
                                last.then_inc(S["y_done"], 1)

                    wait(pe, ("xT_lo_made", SLOT_TILES * e + FIRST[j] + n))
                    for f in range(FT):
                        up(f)
                        if f > 0:
                            down(f - 1)
                        if f in turn_here:
                            i, nj = turn_here[f]
                            nth = FIRST[nj] + i
                            turn_gathered(SLOT_TILES * e + SLOT_TILES * (nj == 0) + nth,
                                          SLOT_TILES // 2 * e + SLOT_TILES // 2 * (nj == 0) + nth // 2 + 1, nj, i)
                    down(FT - 1)

                def spare(j):
                    wait(pe, ("xT_lo_made", SLOT_TILES * (e + 1)))
                    for c in range(FCHUNKS + 2):
                        if c < FCHUNKS:
                            product(h_bank[c % 2][:, :], (xT_hi[j], xT_lo[j]), (w1_hi[c], w1_lo[c]), DT,
                                    slab).then_inc(S["spare_h_done"], 1)
                        if 0 < c <= FCHUNKS:
                            wait(pe, ("spare_h_ready", spare_count(e, j) + c))
                            turn(xt_bank[(c - 1) % 2], xg[:, (c - 1) % 2, :], FPC).then_inc(S["spare_turned"], 1)
                        if c > 1:
                            wait(pe, ("spare_lo_made", spare_count(e, j) + c - 1))
                            if c == 2:
                                banks_read(j)
                            d = c - 2
                            for f in range(FPC):
                                part = slice(f * P, (f + 1) * P)
                                for l, (hx, wx) in enumerate(((h_hi, w2_hi), (h_hi, w2_lo), (h_lo, w2_hi))):
                                    last = mm(y_bank[0][:, :], hx[d % 2][:, part], wx[d][:, f, :],
                                              start=(d == f == l == 0), stop=(d == FCHUNKS - 1 and f == FPC - 1 and l == 2))
                    last.then_inc(S["y_done"], 1)

                expert_blocks(pe, e, main, spare, (("spare_h_done", FCHUNKS), ("spare_turned", FCHUNKS), ("y_done", 1)))

            experts_loop(pe, expert)


_INS = ["L0_attn_x", "L0_attn_log_decay", "L0_attn_Wq", "L0_attn_Wk", "L0_attn_Wv", "L0_attn_Wo", "L0_attn_Wg1",
        "L0_attn_Wg2", "L0_attn_norm_w", "L0_ffn_Wg", "L0_ffn_w1", "L0_ffn_w2"]


def kernel(**inputs):
    import concourse.bacc as _bacc
    from concourse import mybir as _mybir
    from concourse.bass_utils import run_bass_kernel_spmd as _run

    nc = _bacc.Bacc("TRN2", target_bir_lowering=False, num_devices=1)
    arrays, args = {}, []
    for name in _INS:
        a = np.ascontiguousarray(inputs[name])
        arrays[f"in_{name}"] = a
        args.append(nc.dram_tensor(f"in_{name}", a.shape, _mybir.dt.from_np(a.dtype), kind="ExternalInput").ap())
    args.append(nc.dram_tensor("out_rows", (TOKENS + PAD_ROWS, D), F32, kind="ExternalOutput").ap())
    build(nc, *args)
    r = _run(nc, [arrays], core_ids=[0])
    return r.results[0]["out_rows"][:TOKENS].reshape(BATCH, SEQ, D)
```
